# Optimizing a Trainium2 kernel written in Bass

```python
import numpy as np
import jax
import jax.numpy as jnp

def _softmax(x, axis=-1):
    return jax.nn.softmax(x, axis=axis)

def _gelu(x):
    return jax.nn.gelu(x, approximate=True)

def _silu(x):
    return jax.nn.silu(x)

def _sigmoid(x):
    return jax.nn.sigmoid(x)

def _layernorm(x, axis=-1, eps=1e-05):
    m = jnp.mean(x, axis=axis, keepdims=True)
    v = jnp.var(x, axis=axis, keepdims=True)
    return (x - m) / jnp.sqrt(v + eps)

def _scatter_add(tgt, idx, src, axis=0):
    return tgt.at[idx].add(src)

def _segment_sum(src, seg, n):
    return jax.ops.segment_sum(src, seg, n)
kernel_name = 'mk_decoder_preln_d1_seqx_r8_f80703'

def setup_inputs(seed: int=0):
    np.random.seed(seed)
    _w = jnp.asarray

    def _rec_inputs():
        import jax
        import jax.numpy as jnp
        _rk = jax.random.key(seed)
        x = -0.0002928 + 1 * jax.random.normal(jax.random.fold_in(_rk, 1), (2, 256, 128), jnp.float32)
        _lenS = 256 - jax.random.randint(jax.random.fold_in(_rk, 7), (2,), 0, max(1, 256 // 4) + 1, jnp.int32)
        _lenS2 = 512 - jax.random.randint(jax.random.fold_in(_rk, 8), (2,), 0, max(1, 512 // 4) + 1, jnp.int32)
        _ctx_1024P = jax.random.normal(jax.random.fold_in(_rk, 11), (2, 16, 128), jnp.float32)
        _ctx_1024c = jax.random.dirichlet(jax.random.fold_in(_rk, 511), 0.3 * jnp.ones((16,), jnp.float32), (2, 512))
        _ctx_1024t = jnp.einsum('bsk,bkd->bsd', _ctx_1024c, _ctx_1024P)
        _ctx_1024t = _ctx_1024t * jax.lax.rsqrt(jnp.mean(jnp.square(_ctx_1024t)) + 1e-12) * 0.953939
        ctx_1024 = -1.39393e-06 + 0.999914 * (_ctx_1024t + 0.3 * jax.random.normal(jax.random.fold_in(_rk, 611), (2, 512, 128), jnp.float32))
        return (x, ctx_1024)
    x, ctx_1024 = _rec_inputs()

    def _L0_attn_setup():
        import jax, jax.numpy as jnp
        import numpy as np
        B, S, D = (1, 512, 128)
        H, KV, WIN = (8, 2, 32)
        HD = D // H
        FP16_MIN = -65504.0
        key = jax.random.key(seed)
        ks = jax.random.split(key, 10)
        sc = 0.02
        return {'x': jax.random.normal(ks[0], (B, S, D), dtype=jnp.float32), 'sink_bias': jnp.float32(0.0), 'Wq': jax.random.normal(ks[1], (H * HD, D), dtype=jnp.float32) * sc, 'bq': jnp.zeros((H * HD,), dtype=jnp.float32), 'Wk': jax.random.normal(ks[2], (KV * HD, D), dtype=jnp.float32) * sc, 'bk': jnp.zeros((KV * HD,), dtype=jnp.float32), 'Wv': jax.random.normal(ks[3], (KV * HD, D), dtype=jnp.float32) * sc, 'bv': jnp.zeros((KV * HD,), dtype=jnp.float32), 'Wo': jax.random.normal(ks[4], (D, H * HD), dtype=jnp.float32) * sc, 'bo': jnp.zeros((D,), dtype=jnp.float32)}
    _L0_attn_all = _L0_attn_setup()
    _L0_attn_in = {k: v for k, v in _L0_attn_all.items() if k in ('sink_bias', 'Wq', 'bq', 'Wk', 'bk', 'Wv', 'bv', 'Wo', 'bo')}
    del _L0_attn_all

    def _L0_xattn_setup():
        import jax, jax.numpy as jnp
        import numpy as np
        N_HEAD = 16
        key = jax.random.key(seed)
        ks = jax.random.split(key, 7)
        b, lq, lv = (2, 256, 256)
        q_dim = k_dim = v_dim = 128
        s = 0.02
        return {'q': jax.random.normal(ks[0], (b, lq, q_dim), jnp.float32), 'k': jax.random.normal(ks[1], (b, lv, k_dim), jnp.float32), 'v': jax.random.normal(ks[2], (b, lv, v_dim), jnp.float32), 'Wq': jax.random.normal(ks[3], (k_dim, q_dim), jnp.float32) * s, 'Wk': jax.random.normal(ks[4], (k_dim, k_dim), jnp.float32) * s, 'Wv': jax.random.normal(ks[5], (v_dim, v_dim), jnp.float32) * s, 'Wo': jax.random.normal(ks[6], (v_dim, v_dim), jnp.float32) * s}
    _L0_xattn_all = _L0_xattn_setup()
    _L0_xattn_in = {k: v for k, v in _L0_xattn_all.items() if k in ('Wq', 'Wk', 'Wv', 'Wo')}
    del _L0_xattn_all

    def _L0_ffn_setup():
        import jax, jax.numpy as jnp
        import numpy as np
        ALPHA = 1.702
        LIMIT = 7.0
        TOP_K = 2
        key = jax.random.key(seed)
        ks = jax.random.split(key, 4)
        B, S, H, E, I = (2, 128, 128, 8, 256)
        return {'hidden_states': jax.random.normal(ks[0], (B, S, H), jnp.float32), 'router_weight': jax.random.normal(ks[1], (E, H), jnp.float32), 'router_bias': jnp.zeros((E,), jnp.float32), 'gate_up_proj': jax.random.normal(ks[2], (E, H, 2 * I), jnp.float32) * 0.02, 'gate_up_bias': jnp.zeros((E, 2 * I), jnp.float32), 'down_proj': jax.random.normal(ks[3], (E, I, H), jnp.float32) * 0.02, 'down_bias': jnp.zeros((E, H), jnp.float32)}
    _L0_ffn_all = _L0_ffn_setup()
    _L0_ffn_in = {k: v for k, v in _L0_ffn_all.items() if k in ('router_weight', 'router_bias', 'gate_up_proj', 'gate_up_bias', 'down_proj', 'down_bias')}
    del _L0_ffn_all
    return {'x': x, 'ctx_1024': ctx_1024, 'L0_attn_sink_bias': _L0_attn_in['sink_bias'], 'L0_attn_Wq': _L0_attn_in['Wq'], 'L0_attn_bq': _L0_attn_in['bq'], 'L0_attn_Wk': _L0_attn_in['Wk'], 'L0_attn_bk': _L0_attn_in['bk'], 'L0_attn_Wv': _L0_attn_in['Wv'], 'L0_attn_bv': _L0_attn_in['bv'], 'L0_attn_Wo': _L0_attn_in['Wo'], 'L0_attn_bo': _L0_attn_in['bo'], 'L0_xattn_Wq': _L0_xattn_in['Wq'], 'L0_xattn_Wk': _L0_xattn_in['Wk'], 'L0_xattn_Wv': _L0_xattn_in['Wv'], 'L0_xattn_Wo': _L0_xattn_in['Wo'], 'L0_ffn_router_weight': _L0_ffn_in['router_weight'], 'L0_ffn_router_bias': _L0_ffn_in['router_bias'], 'L0_ffn_gate_up_proj': _L0_ffn_in['gate_up_proj'], 'L0_ffn_gate_up_bias': _L0_ffn_in['gate_up_bias'], 'L0_ffn_down_proj': _L0_ffn_in['down_proj'], 'L0_ffn_down_bias': _L0_ffn_in['down_bias']}

def reference(x, ctx_1024, L0_attn_sink_bias, L0_attn_Wq, L0_attn_bq, L0_attn_Wk, L0_attn_bk, L0_attn_Wv, L0_attn_bv, L0_attn_Wo, L0_attn_bo, L0_xattn_Wq, L0_xattn_Wk, L0_xattn_Wv, L0_xattn_Wo, L0_ffn_router_weight, L0_ffn_router_bias, L0_ffn_gate_up_proj, L0_ffn_gate_up_bias, L0_ffn_down_proj, L0_ffn_down_bias):
    import jax
    import jax.numpy as jnp

    def _L0_attn_ref(x, sink_bias, Wq, bq, Wk, bk, Wv, bv, Wo, bo):
        import jax, jax.numpy as jnp
        import numpy as np
        B, S, D = (1, 512, 128)
        H, KV, WIN = (8, 2, 32)
        HD = D // H
        FP16_MIN = -65504.0
        b, s, d = x.shape
        q = (x @ Wq.T + bq).reshape(b, s, H, HD).transpose(0, 2, 1, 3)
        k = (x @ Wk.T + bk).reshape(b, s, KV, HD).transpose(0, 2, 1, 3)
        v = (x @ Wv.T + bv).reshape(b, s, KV, HD).transpose(0, 2, 1, 3)
        k = jnp.repeat(k, H // KV, axis=1)
        v = jnp.repeat(v, H // KV, axis=1)
        scores = jnp.einsum('bhqd,bhkd->bhqk', q, k) / jnp.sqrt(jnp.float32(HD))
        i = jnp.arange(s)[:, None]
        j = jnp.arange(s)[None, :]
        mask = (j <= i) & (j > i - WIN)
        scores = jnp.where(mask, scores, FP16_MIN)
        m = jnp.maximum(scores.max(axis=-1, keepdims=True), sink_bias)
        e = jnp.exp(scores - m)
        sink = jnp.exp(sink_bias - m)
        attn = e / (e.sum(axis=-1, keepdims=True) + sink)
        out = jnp.einsum('bhqk,bhkd->bhqd', attn, v)
        out = out.transpose(0, 2, 1, 3).reshape(b, s, H * HD)
        return out @ Wo.T + bo

    def _L0_xattn_ref(q, k, v, Wq, Wk, Wv, Wo):
        import jax, jax.numpy as jnp
        import numpy as np
        N_HEAD = 16
        b, lq, _ = q.shape
        lv = k.shape[1]
        qp = q @ Wq.T
        kp = k @ Wk.T
        vp = v @ Wv.T
        qh = qp.reshape(b, lq, N_HEAD, -1).transpose(0, 2, 1, 3)
        kh = kp.reshape(b, lv, N_HEAD, -1).transpose(0, 2, 1, 3)
        vh = vp.reshape(b, lv, N_HEAD, -1).transpose(0, 2, 1, 3)
        d = qh.shape[-1]
        scores = jnp.einsum('bhqd,bhkd->bhqk', qh, kh) / jnp.sqrt(jnp.float32(d))
        p = jax.nn.softmax(scores, axis=-1)
        attn = jnp.einsum('bhqk,bhkd->bhqd', p, vh)
        attn = attn.transpose(0, 2, 1, 3).reshape(b, lq, -1)
        return attn @ Wo.T

    def _L0_ffn_ref(hidden_states, router_weight, router_bias, gate_up_proj, gate_up_bias, down_proj, down_bias):
        import jax, jax.numpy as jnp
        import numpy as np
        ALPHA = 1.702
        LIMIT = 7.0
        TOP_K = 2
        B, S, H = hidden_states.shape
        E, _, two_I = gate_up_proj.shape
        I = two_I // 2
        flat = hidden_states.reshape(B * S, H)
        logits = flat @ router_weight.T + router_bias
        scores = jax.nn.softmax(logits, axis=-1)
        topk_w, topk_idx = jax.lax.top_k(scores, TOP_K)
        gu = jnp.einsum('th,ehn->ten', flat, gate_up_proj) + gate_up_bias
        gate = jnp.minimum(gu[..., :I], LIMIT)
        up = jnp.clip(gu[..., I:], -LIMIT, LIMIT)
        glu = gate * jax.nn.sigmoid(gate * ALPHA)
        act = (up + 1.0) * glu
        down = jnp.einsum('tei,eih->teh', act, down_proj) + down_bias
        gathered = jnp.take_along_axis(down, topk_idx[:, :, None], axis=1)
        out = (gathered * topk_w[:, :, None]).sum(axis=1)
        return out.reshape(B, S, H)
    x = x + _L0_attn_ref(_layernorm(x, axis=-1), L0_attn_sink_bias, L0_attn_Wq, L0_attn_bq, L0_attn_Wk, L0_attn_bk, L0_attn_Wv, L0_attn_bv, L0_attn_Wo, L0_attn_bo)
    x = x + _L0_xattn_ref(_layernorm(x, axis=-1), ctx_1024, ctx_1024, L0_xattn_Wq, L0_xattn_Wk, L0_xattn_Wv, L0_xattn_Wo)
    x = x + _L0_ffn_ref(_layernorm(x, axis=-1), L0_ffn_router_weight, L0_ffn_router_bias, L0_ffn_gate_up_proj, L0_ffn_gate_up_bias, L0_ffn_down_proj, L0_ffn_down_bias)
    return x

_drawn_inputs = setup_inputs


def setup_inputs(seed=0):
    import zlib

    import numpy as np

    out = dict(_drawn_inputs(seed))
    spreads = {'L0_attn_bq': (0.0, 0.8),
     'L0_attn_bk': (0.0, 2.0),
     'L0_attn_bv': (0.0, 0.338),
     'L0_attn_bo': (0.0, 0.1),
     'L0_ffn_router_bias': (0.0, 2.0),
     'L0_ffn_gate_up_bias': (0.0, 0.495),
     'L0_ffn_down_bias': (0.0, 0.1)}
    factors = {'L0_attn_Wq': 8.0,
     'L0_attn_Wk': 8.0,
     'L0_attn_Wv': 5.784,
     'L0_xattn_Wq': 8.0,
     'L0_xattn_Wk': 8.0}
    for name, (base, spread) in spreads.items():
        noise = np.random.default_rng([zlib.crc32(name.encode()), seed]).standard_normal(out[name].shape)
        drawn = base * np.exp(spread * noise) if base else spread * noise
        out[name] = jnp.asarray(drawn.astype(out[name].dtype))
    for name, factor in factors.items():
        out[name] = (out[name] * factor).astype(out[name].dtype)
    return out
```

```python
import numpy as np
import concourse.bass as bass
from concourse import mybir
from contextlib import ExitStack

P = 128
B, S, D = 2, 256, 128
T = B * S
NT = T // P
SK = 512
NKT = SK // P
H1, KV, HD1, WIN = 8, 2, 16, 32
H2, HD2 = 16, 8
NE, FI = 8, 256
NC = FI // P
TERMS = 6
STACK = 64
NM_ROW = HD2 * TERMS
NPAIR = H2 // 2
QUADS = 4
UNITS = B * QUADS
EPS = 1e-5
MASKED = -1e30
STRIP = (P, P + WIN)
HB = (4, 3)
VW = P + HD1
Q_PARTS = (0, 0, 0, 1, 1, 2)
K_PARTS = (0, 1, 2, 0, 1, 0)

PACK1 = dict(wq=P, wk=P, wv=KV * HD1, wo=P, ident=P, bq=1, bk=1, sink=1, bv=KV * HD1, bo=D, head=H1)
PACK2 = dict(wq=P, wk=P, wv=P, wo=P, wr=NE, br=NE, gub=4 * NE, iota=NE)


def columns(pack):
    at, out = 0, {}
    for name, n in pack.items():
        out[name] = (at, at + n)
        at += n
    return out, at


def build(nc, x, ctxT, pack1, pack2, maskc, gu, dn, db, out):
    fp32, bf16, u32 = mybir.dt.float32, mybir.dt.bfloat16, mybir.dt.uint32
    ALU, ACT, AX = mybir.AluOpType, mybir.ActivationFunctionType, mybir.AxisListType
    c1, n1 = columns(PACK1)
    c2, n2 = columns(PACK2)

    with ExitStack() as ctx:
        def sb(name, shape, dt=fp32):
            return ctx.enter_context(nc.sbuf_tensor(name, shape, dt))

        def sem(name):
            return ctx.enter_context(nc.semaphore(name))

        xs = sb("xs", [P, NT, D])
        xbo = sb("xbo", [P, NT, D])
        w1 = sb("w1", [P, n1])
        w2 = sb("w2", [P, n2])
        msk = sb("msk", [P, 4 * P + 3 * STRIP[1] + P], bf16)
        ctx_sb = sb("ctx_sb", [P, B * SK])
        db_sb = sb("db_sb", [NE, D])
        stats = sb("stats", [P, 3, NT, 6])
        mv = sb("mv", [P, 3, NT, 2])
        veps = sb("veps", [P, 3, NT])
        mhalf = sb("mhalf", [P, NT])
        rstd = sb("rstd", [P, 3, NT])
        xn = sb("xn", [P, 3, NT, D])
        xnT = sb("xnT", [P, 3, T])
        qT = sb("qT", [P, T])
        kT = sb("kT", [P, T])
        vspill = sb("vspill", [WIN, B, H1 * VW])
        negm1 = sb("negm1", [P, NT, H1])
        rmax1 = sb("rmax1", [P, NT, H1])
        sums1 = sb("sums1", [P, NT, H1])
        esink = sb("esink", [P, NT, H1])
        den1 = sb("den1", [P, NT, H1])
        rden1 = sb("rden1", [P, NT, H1])
        pn1 = sb("pn1", [P, 2, H1, STRIP[1]])
        pT1 = sb("pT1", [P, 2, H1, P])
        pTs = sb("pTs", [WIN, H1, WIN])
        oT1 = sb("oT1", [P, 2, P])
        x1 = sb("x1", [P, NT, D])
        kparts = sb("kparts", [P, TERMS, B * SK], bf16)
        kres = sb("kres", [P, B * SK])
        qparts = sb("qparts", [P, TERMS, T], bf16)
        qres = sb("qres", [P, T])
        kst = sb("kst", [P, NPAIR, B * SK], bf16)
        qst = sb("qst", [P, NPAIR, B, 2, S], bf16)
        vaug = sb("vaug", [P, B * NKT, H2, 32])
        m2 = sb("m2", [P, NT, H2])
        nms = sb("nms", [4, 2, S])
        nmp = sb("nmp", [4, 2, 3, S], bf16)
        pT2 = sb("pT2", [P, 2, NKT, 4, S])
        oq = sb("oq", [P, 2, S])
        rs2 = sb("rs2", [P, NT, H2])
        o2 = xs
        o2T = sb("o2T", [P, NT, P])
        x2 = sb("x2", [P, NT, D])
        lg = sb("lg", [P, NT, NE])
        lmax = sb("lmax", [P, NT])
        ex = sb("ex", [P, NT, NE])
        esum = sb("esum", [P, NT])
        rsum = sb("rsum", [P, NT])
        sc = sb("sc", [P, NT, NE])
        top = sb("top", [P, NT, 8])
        topi = sb("topi", [P, NT, 8], u32)
        topf = sb("topf", [P, NT, 8])
        hit = sb("hit", [P, 2, NT, NE])
        hw = sb("hw", [P, 2, NT, NE])
        cw = sb("cw", [P, NT, NE])
        cwT = sb("cwT", [NE, T])
        spare = pT2[:, :, :, :, :].rearrange("p a b c d -> p (a b c d)")
        g1, sg, u1, u2, glu = (spare[:, 2 * T * k:2 * T * (k + 1)].rearrange("p (n t) -> p n t", n=2) for k in range(5))
        act_sb = spare[:, 10 * T:14 * T].rearrange("p (n c t) -> p n c t", n=2, c=NC)
        kexp = spare[:, 0:H1 * T].rearrange("p (h t) -> p h t", h=H1)
        p1 = spare[:, H1 * T:H1 * T + 2 * H1 * STRIP[1]].rearrange("p (n h j) -> p n h j", n=2, h=H1)
        wexp = sb("wexp", [P, NE * 2 * FI + NE * NC * D])
        gu_sb = wexp[:, 0:NE * 2 * FI].rearrange("p (e n) -> p e n", e=NE)
        dn_sb = wexp[:, NE * 2 * FI:].rearrange("p (e c d) -> p e c d", e=NE, c=NC)
        vpad = wexp[:, 0:NT * H1 * VW].rearrange("p (t n) -> p t n", t=NT)
        acc = xbo

        wcol = lambda name: w1[:, c1[name][0]:c1[name][1]]
        xcol = lambda name: w2[:, c2[name][0]:c2[name][1]]
        identf = wcol("ident")
        mask_at = (msk[:, 0:4 * P], msk[:, 4 * P:4 * P + 3 * STRIP[1]])
        identb = msk[:, 4 * P + 3 * STRIP[1]:]

        ps = ctx.enter_context(nc.psum_tensor("ps", [P, 8, 512], fp32))
        psb = lambda b: ps[:, b, :]

        d_x, d_w1, d_msk, d_ctx, d_w2, d_gu, d_dn = (sem(n) for n in
                                                     ("d_x", "d_w1", "d_msk", "d_ctx", "d_w2", "d_gu", "d_dn"))
        d_kst = sem("d_kst")
        d_qst = [sem(f"d_qst{b}") for b in range(B)]
        d_nm = [sem(f"d_nm{u}") for u in range(UNITS)]
        d_out = sem("d_out")
        zeroed = sem("zeroed")
        chain = sem("chain")
        kmid_ready = sem("kmid_ready")
        var_ready, rstd_ready, xn_ready, xbo_ready = sem("var_ready"), sem("rstd_ready"), sem("xn_ready"), sem("xbo_ready")
        xnT_ps, xnT_ready = sem("xnT_ps"), sem("xnT_ready")
        kv2_ps = sem("kv2_ps")
        khi_ready, kres_ready, kparts_ready, vaug_ready = (sem("khi_ready"), sem("kres_ready"), sem("kparts_ready"), sem("vaug_ready"))
        qkv1_ps = sem("qkv1_ps")
        qT_ready, kT_ready, kexp_ready, vpad_ready = sem("qT_ready"), sem("kT_ready"), sem("kexp_ready"), sem("vpad_ready")
        s1_ps, negm1_ready, p1_ready, esink_ready, pn1_ready = (sem("s1_ps"), sem("negm1_ready"), sem("p1_ready"), sem("esink_ready"), sem("pn1_ready"))
        spill_ready = sem("spill_ready")
        pT1_ps, pT1a_ready, pT1b_ready = sem("pT1_ps"), sem("pT1a_ready"), sem("pT1b_ready")
        o1_ps, oT1_ready, y1_ps, x1_ready = sem("o1_ps"), sem("oT1_ready"), sem("y1_ps"), sem("x1_ready")
        q2_ps, qhi_ready, qres_ready, qparts_ready = sem("q2_ps"), sem("qhi_ready"), sem("qres_ready"), sem("qparts_ready")
        s2_ps, m2_ready = sem("s2_ps"), sem("m2_ready")
        mT_ps, nmp_ready = sem("mT_ps"), sem("nmp_ready")
        st_ps, p2_ready = sem("st_ps"), sem("p2_ready")
        pv_ps, oq_ready, oqT_ps, o2_ready = sem("pv_ps"), sem("oq_ready"), sem("oqT_ps"), sem("o2_ready")
        o2T_ps, o2T_ready, y2_ps, x2_ready = sem("o2T_ps"), sem("o2T_ready"), sem("y2_ps"), sem("x2_ready")
        lg_ps, lg_ready, ex_ready, cw_ready = sem("lg_ps"), sem("lg_ready"), sem("ex_ready"), sem("cw_ready")
        cwT_ps, cwT_ready, db_ps, acc_ready = sem("cwT_ps"), sem("cwT_ready"), sem("db_ps"), sem("acc_ready")
        g_ps, u_ps, g1_ready, sg_ready, u1_ready = sem("g_ps"), sem("u_ps"), sem("g1_ready"), sem("sg_ready"), sem("u1_ready")
        u2_ready, glu_ready, act_ready, dn_ps, dn_used = (sem("u2_ready"), sem("glu_ready"), sem("act_ready"), sem("dn_ps"), sem("dn_used"))

        block = ctx.enter_context(nc.Block())
        heads_of_bank = lambda k: [(i, min(i + HB[k], H1)) for i in range(0, H1, HB[k])]
        s1_bank = lambda t: 3 * (t % 2)
        O1, M7 = 6, 7
        unit = lambda u: (u // QUADS, u % QUADS)

        @block.sync
        def _(sp):
            sp.dma_start(xs[:, :, :], x.rearrange("(t p) d -> p t d", p=P)).then_inc(d_x, 16)
            sp.dma_start(w1[:, :], pack1).then_inc(d_w1, 16)
            sp.dma_start(msk[:, :], maskc).then_inc(d_msk, 16)
            sp.wait_ge(khi_ready, 2)
            sp.wait_ge(kmid_ready, 1)
            sp.wait_ge(kparts_ready, 4)
            sp.wait_ge(zeroed, 6)
            for h in range(H2):
                r = STACK * (h % 2)
                sp.dma_start(kst[r:r + NM_ROW, h // 2, :], kparts[h * HD2:(h + 1) * HD2, :, :]).then_inc(d_kst, 16)
            for b in range(B):
                sp.wait_ge(qparts_ready, 3 * (b + 1))
                for h in range(H2):
                    r = STACK * (h % 2)
                    sp.dma_start(qst[r:r + NM_ROW, h // 2, b, h % 2, :],
                                 qparts[h * HD2:(h + 1) * HD2, :, b * S:(b + 1) * S]).then_inc(d_qst[b], 16)
                if b == 1:
                    sp.wait_ge(x1_ready, NT)
                    sp.dma_start(gu_sb[:, :, :], gu.rearrange("e p n -> p e n")).then_inc(d_gu, 16)
                    sp.dma_start(dn_sb[:, :, :, :], dn.rearrange("e (c p) d -> p e c d", p=P)).then_inc(d_dn, 16)
                    sp.dma_start(db_sb[:, :], db).then_inc(d_dn, 16)
            for u in range(UNITS):
                b, quad = unit(u)
                sp.wait_ge(nmp_ready, u + 1)
                sp.wait_ge(s2_ps, 4 * (u + 1))
                for k in range(4):
                    h = 4 * quad + k
                    r = STACK * (h % 2) + NM_ROW
                    sp.dma_start(qst[r:r + 3, h // 2, b, h % 2, :], nmp[k:k + 1, u % 2, :, :]).then_inc(d_nm[u], 16)
            sp.wait_ge(acc_ready, NT)
            sp.dma_start(out.rearrange("(t p) d -> p t d", p=P), acc[:, :, :]).then_inc(d_out, 16)
            sp.wait_ge(d_out, 16)

        @block.gpsimd
        def _(pool):
            nc.gpsimd.memset(mhalf[:, :], -0.5).then_inc(zeroed, 1)
            nc.gpsimd.memset(vpad[:, :, :], 0.0).then_inc(zeroed, 1)
            nc.gpsimd.memset(vspill[:, :, :], 0.0).then_inc(zeroed, 1)
            pool.wait_ge(var_ready, 1)
            pool.wait_ge(zeroed, 3)
            nc.gpsimd.tensor_tensor(rstd[:, 0, :], veps[:, 0, :], mhalf[:, :], ALU.pow).then_inc(rstd_ready, 1)
            nc.gpsimd.memset(qst[:, :, :, :, :], 0.0).then_inc(zeroed, 1)
            nc.gpsimd.memset(kst[:, :, :], 1.0).then_inc(zeroed, 1)
            nc.gpsimd.memset(vaug[:, :, :, :], 0.0).then_inc(zeroed, 1)
            pool.wait_ge(zeroed, 6)
            nc.gpsimd.memset(vaug[:, :, :, HD2:HD2 + 1], 1.0).then_inc(zeroed, 1)
            pool.wait_ge(d_x, 16)
            pool.wait_ge(d_w1, 16)
            nc.gpsimd.tensor_tensor(xbo[:, :, :], xs[:, :, :], wcol("bo").unsqueeze(1).to_broadcast([P, NT, D]), ALU.add).then_inc(xbo_ready, 1)
            pool.wait_ge(kres_ready, 1)
            nc.gpsimd.tensor_copy(kparts[:, 1, :], kres[:, :]).then_inc(kmid_ready, 1)
            nc.gpsimd.tensor_copy(kparts[:, 4, :], kres[:, :]).then_inc(kparts_ready, 1)
            pool.wait_ge(kmid_ready, 1)
            nc.gpsimd.tensor_tensor(kparts[:, 2, :], kres[:, :], kparts[:, 1, :], ALU.subtract).then_inc(kparts_ready, 1)
            for b in range(B):
                pool.wait_ge(var_ready, 2 + b)
                nc.gpsimd.tensor_tensor(rstd[:, 1, 2 * b:2 * b + 2], veps[:, 1, 2 * b:2 * b + 2], mhalf[:, 0:2], ALU.pow).then_inc(rstd_ready, 1)
            pool.wait_ge(var_ready, 4)
            nc.gpsimd.tensor_tensor(rstd[:, 2, :], veps[:, 2, :], mhalf[:, :], ALU.pow).then_inc(rstd_ready, 1)
            for n in range(NE * NC):
                pool.wait_ge(sg_ready, n + 1)
                if n >= 2:
                    pool.wait_ge(act_ready, n - 1)
                nc.gpsimd.tensor_tensor(glu[:, n % 2, :], g1[:, n % 2, :], sg[:, n % 2, :], ALU.mult).then_inc(glu_ready, 1)

        @block.scalar
        def _(act):
            act.dma_start(ctx_sb[:, :], ctxT).then_inc(d_ctx, 16)
            act.dma_start(w2[:, :], pack2).then_inc(d_w2, 16)
            act.wait_ge(kv2_ps, 1)
            for c in range(2):
                nc.scalar.activation(kparts[:, 0, c * 512:(c + 1) * 512], psb(2 + c), ACT.Copy).then_inc(khi_ready, 1)
            act.wait_ge(kres_ready, 1)
            for j, term in enumerate((3, 5)):
                nc.scalar.activation(kparts[:, term, :], kparts[:, 0, :], ACT.Copy).then_inc(kparts_ready, 1)
            act.wait_ge(khi_ready, 2)
            act.wait_ge(kv2_ps, 2)
            act.wait_ge(zeroed, 7)
            for c in range(2):
                nc.scalar.activation(vaug[:, 4 * c:4 * c + 4, :, 0:HD2],
                                     psb(4 + c).rearrange("p (t h d) -> p t h d", t=4, d=HD2), ACT.Copy).then_inc(vaug_ready, 1)
            act.wait_ge(xnT_ps, 1)
            nc.scalar.activation(xnT[:, 0, :], psb(O1), ACT.Copy).then_inc(xnT_ready, 1)
            act.wait_ge(qkv1_ps, 2)
            nc.scalar.activation(kT[:, :], psb(0), ACT.Identity, bias=wcol("bk")).then_inc(kT_ready, 1)

            def softmax1(t):
                k = t % 2
                act.wait_ge(negm1_ready, t + 1)
                for i, (h0, h1) in enumerate(heads_of_bank(k)):
                    for h in range(h0, h1):
                        src = ps[:, s1_bank(t) + i, (h - h0) * STRIP[k]:(h - h0 + 1) * STRIP[k]]
                        if t >= 2 and h == 0:
                            act.wait_ge(pn1_ready, t - 1)
                        nc.scalar.activation(p1[:, k, h, 0:STRIP[k]], src, ACT.Exp, bias=negm1[:, t, h:h + 1],
                                             accum_out=sums1[:, t, h:h + 1]).then_inc(p1_ready, 1)
                nc.scalar.activation(esink[:, t, :], negm1[:, t, :], ACT.Exp, bias=wcol("sink")).then_inc(esink_ready, 1)

            def pT1_half(t):
                act.wait_ge(pT1_ps, t + 1)
                if t >= 2:
                    act.wait_ge(o1_ps, t - 1)
                nc.scalar.activation(pT1[:, t % 2, 0:4, :], psb(s1_bank(t)).rearrange("p (h q) -> p h q", h=4), ACT.Copy).then_inc(pT1a_ready, 1)
                act.wait_ge(o1_ps, t + 1)
                if t >= 2:
                    act.wait_ge(y1_ps, t - 1)
                nc.scalar.activation(oT1[:, t % 2, :], ps[:, O1, 0:P], ACT.Copy).then_inc(oT1_ready, 1)

            def queries2(b):
                cols = slice(b * S, (b + 1) * S)
                act.wait_ge(xnT_ps, 2 + b)
                nc.scalar.activation(xnT[:, 1, cols], ps[:, M7, 0:S], ACT.Copy).then_inc(xnT_ready, 1)
                act.wait_ge(q2_ps, b + 1)
                nc.scalar.activation(qparts[:, 0:3, cols], ps[:, M7, 0:S].unsqueeze(1).to_broadcast([P, 3, S]), ACT.Copy).then_inc(qhi_ready, 1)

            softmax1(0)
            softmax1(1)
            pT1_half(0)
            softmax1(2)
            pT1_half(1)
            softmax1(3)
            queries2(0)
            pT1_half(2)
            pT1_half(3)
            queries2(1)

            def out_quad(u):
                act.wait_ge(pv_ps, u + 1)
                if u >= 2:
                    act.wait_ge(oqT_ps, u - 1)
                nc.scalar.activation(oq[:, u % 2, :], ps[:, 6, 0:S], ACT.Copy).then_inc(oq_ready, 1)

            for i in range(UNITS + 1):
                if i < UNITS:
                    for n in range(8 * i, 8 * i + 8):
                        kt, pair = n % 8 // 2, n % 2
                        act.wait_ge(st_ps, n + 1)
                        if i >= 2:
                            act.wait_ge(pv_ps, i - 1)
                        nc.scalar.activation(pT2[:, i % 2, kt, 2 * pair:2 * pair + 2, :],
                                             psb(4 + n % 2).rearrange("p (s q) -> p s q", s=2), ACT.Exp,
                                             scale=float(HD2) ** -0.5).then_inc(p2_ready, 1)
                        if n == 8 * i + 7 and i >= 1:
                            out_quad(i - 1)
                else:
                    out_quad(i - 1)
            for t in range(NT):
                act.wait_ge(o2T_ps, t + 1)
                nc.scalar.activation(o2T[:, t, :], ps[:, t, 0:P], ACT.Copy).then_inc(o2T_ready, 1)
            act.wait_ge(xnT_ps, 4)
            nc.scalar.activation(xnT[:, 2, :], psb(4), ACT.Copy).then_inc(xnT_ready, 1)
            act.wait_ge(lg_ready, 1)
            nc.scalar.activation(ex[:, :, :], lg[:, :, :], ACT.Exp).then_inc(ex_ready, 1)

            for n in range(NE * NC):
                e, c = n // NC, n % NC
                bias_u = w2[:, c2["gub"][0] + 4 * e + NC + c:c2["gub"][0] + 4 * e + NC + c + 1]
                act.wait_ge(u_ps, n + 1)
                if n >= 2:
                    act.wait_ge(u2_ready, n - 1)
                nc.scalar.activation(u1[:, n % 2, :], psb(2 + n % 2), ACT.Identity, bias=bias_u).then_inc(u1_ready, 1)
                act.wait_ge(g1_ready, n + 1)
                if n >= 2:
                    act.wait_ge(glu_ready, n - 1)
                nc.scalar.activation(sg[:, n % 2, :], g1[:, n % 2, :], ACT.Sigmoid, scale=1.702).then_inc(sg_ready, 1)

        @block.vector
        def _(dve):
            links = [0]

            def link(ins):
                links[0] += 1
                ins.then_inc(chain, 1)
                dve.wait_ge(chain, links[0])

            def normalise(n, src, tiles, k):
                for t in tiles:
                    last = nc.vector.bn_stats(stats[:, n, t, :], src[:, t, :])
                    links[0] += 1
                    last.then_inc(chain, 1)
                dve.wait_ge(chain, links[0])
                for t in tiles:
                    last = nc.vector.bn_aggr(mv[:, n, t, :], stats[:, n, t, :])
                link(last)
                tt = slice(tiles[0], tiles[-1] + 1)
                nc.vector.tensor_scalar(veps[:, n, tt], mv[:, n, tt, 1], EPS, None, ALU.add).then_inc(var_ready, 1)
                dve.wait_ge(rstd_ready, k)
                for t in tiles:
                    nc.vector.tensor_scalar(xn[:, n, t, :], src[:, t, :], mv[:, n, t, 0:1], rstd[:, n, t:t + 1],
                                            ALU.subtract, ALU.mult).then_inc(xn_ready, 1)

            dve.wait_ge(d_x, 16)
            normalise(0, xs, range(NT), 1)

            dve.wait_ge(khi_ready, 2)
            link(nc.vector.tensor_tensor(kres[:, 0:512], psb(2), kparts[:, 0, 0:512], ALU.subtract))
            nc.vector.tensor_tensor(kres[:, 512:1024], psb(3), kparts[:, 0, 512:1024], ALU.subtract).then_inc(kres_ready, 1)

            dve.wait_ge(d_w1, 16)
            dve.wait_ge(qkv1_ps, 1)
            nc.vector.tensor_scalar(qT[:, :], psb(M7), wcol("bq"), float(HD1) ** -0.5, ALU.add, ALU.mult).then_inc(qT_ready, 1)
            dve.wait_ge(kT_ready, 1)
            for h in range(H1):
                nc.vector.tensor_scalar(kexp[:, h, :], kT[:, :], w1[:, c1["head"][0] + h:c1["head"][0] + h + 1], None, ALU.mult).then_inc(kexp_ready, 1)
            dve.wait_ge(qkv1_ps, 3)
            dve.wait_ge(zeroed, 3)
            bv4 = lambda n: w1[0:n, c1["bv"][0]:c1["bv"][1]].rearrange("p (g d) -> p g d", g=KV).unsqueeze(2).to_broadcast([n, KV, H1 // KV, HD1])
            spread = lambda v: v.rearrange("p (g r c) -> p g r c", g=KV, c=VW)[:, :, :, 0:HD1]
            for t in range(NT):
                src = ps[:, 1, t * 32:(t + 1) * 32].rearrange("p (g d) -> p g d", g=KV).unsqueeze(2).to_broadcast([P, KV, H1 // KV, HD1])
                nc.vector.tensor_tensor(spread(vpad[:, t, :]), src, bv4(P), ALU.add).then_inc(vpad_ready, 1)
            for b in range(B):
                src = ps[0:WIN, 1, 128 + b * 32:128 + (b + 1) * 32].rearrange("p (g d) -> p g d", g=KV).unsqueeze(2).to_broadcast([WIN, KV, H1 // KV, HD1])
                nc.vector.tensor_tensor(spread(vspill[:, b, :]), src, bv4(WIN), ALU.add).then_inc(vpad_ready, 1)

            def maxima1(t):
                k = t % 2
                dve.wait_ge(s1_ps, t + 1)
                if k == 0:
                    link(nc.vector.tensor_reduce(rmax1[:, t, :], ps[:, s1_bank(t):s1_bank(t) + 2, :].rearrange("p b (h j) -> p (b h) j", h=4), AX.X, ALU.max))
                else:
                    a = s1_bank(t)
                    nc.vector.tensor_reduce(rmax1[:, t, 0:6].rearrange("p (b h) -> p b h", b=2),
                                            ps[:, a:a + 2, 0:3 * STRIP[1]].rearrange("p b (h j) -> p b h j", h=3), AX.X, ALU.max)
                    links[0] += 0
                    link(nc.vector.tensor_reduce(rmax1[:, t, 6:8], ps[:, a + 2, 0:2 * STRIP[1]].rearrange("p (h j) -> p h j", h=2), AX.X, ALU.max))
                nc.vector.tensor_scalar(negm1[:, t, :], rmax1[:, t, :], wcol("sink"), -1.0, ALU.max, ALU.mult).then_inc(negm1_ready, 1)

            def normalise_p(t):
                k = t % 2
                dve.wait_ge(p1_ready, H1 * (t + 1))
                dve.wait_ge(esink_ready, t + 1)
                link(nc.vector.tensor_tensor(den1[:, t, :], sums1[:, t, :], esink[:, t, :], ALU.add))
                link(nc.vector.reciprocal(rden1[:, t, :], den1[:, t, :]))
                if t >= 2:
                    dve.wait_ge(pT1_ps, t - 1)
                nc.vector.tensor_tensor(pn1[:, k, :, 0:STRIP[k]], p1[:, k, :, 0:STRIP[k]],
                                        rden1[:, t, :].unsqueeze(2).to_broadcast([P, H1, STRIP[k]]), ALU.mult).then_inc(pn1_ready, 1)
                if k == 1:
                    dve.wait_ge(pn1_ready, t + 1)
                    if t == 3:
                        dve.wait_ge(o1_ps, 2)
                    nc.vector.transpose(pTs[:, :, :], pn1[0:WIN, 1, :, 0:WIN]).then_inc(spill_ready, 1)

            def pT1_half(t):
                dve.wait_ge(pT1_ps, t + 1)
                if t >= 2:
                    dve.wait_ge(o1_ps, t - 1)
                nc.vector.tensor_copy(pT1[:, t % 2, 4:8, :], psb(s1_bank(t) + 1).rearrange("p (h q) -> p h q", h=4)).then_inc(pT1b_ready, 1)

            def residual1(t):
                dve.wait_ge(y1_ps, t + 1)
                dve.wait_ge(xbo_ready, 1)
                nc.vector.tensor_tensor(x1[:, t, :], ps[:, O1, P:2 * P], xbo[:, t, :], ALU.add).then_inc(x1_ready, 1)

            def queries2(b):
                dve.wait_ge(x1_ready, 2 * b + 2)
                normalise(1, x1, range(2 * b, 2 * b + 2), 2 + b)
                cols = slice(b * S, (b + 1) * S)
                dve.wait_ge(qhi_ready, b + 1)
                link(nc.vector.tensor_tensor(qres[:, cols], ps[:, M7, 0:S], qparts[:, 0, cols], ALU.subtract))
                qres_ready_n[0] += 1
                nc.vector.tensor_copy(qparts[:, 3, cols], qres[:, cols]).then_inc(qparts_ready, 1)
                nc.vector.tensor_copy(qparts[:, 4, cols], qres[:, cols]).then_inc(qparts_ready, 1)
                dve.wait_ge(qparts_ready, 3 * b + 2)
                nc.vector.tensor_tensor(qparts[:, 5, cols], qres[:, cols], qparts[:, 3, cols], ALU.subtract).then_inc(qparts_ready, 1)

            qres_ready_n = [0]
            maxima1(0)
            maxima1(1)
            normalise_p(0)
            pT1_half(0)
            normalise_p(1)
            residual1(0)
            maxima1(2)
            pT1_half(1)
            residual1(1)
            maxima1(3)
            queries2(0)
            normalise_p(2)
            pT1_half(2)
            normalise_p(3)
            residual1(2)
            pT1_half(3)
            residual1(3)
            queries2(1)

            def split_max(u):
                dve.wait_ge(mT_ps, u + 1)
                if u >= 1:
                    dve.wait_ge(nmp_ready, u)
                if u >= 2:
                    dve.wait_ge(d_nm[u - 2], 16 * 4)
                link(nc.vector.tensor_scalar(nms[:, 0, :], ps[0:4, M7, 0:S], -1.0, None, ALU.mult))
                link(nc.vector.tensor_copy(nmp[:, u % 2, 0, :], nms[:, 0, :]))
                link(nc.vector.tensor_tensor(nms[:, 1, :], nms[:, 0, :], nmp[:, u % 2, 0, :], ALU.subtract))
                link(nc.vector.tensor_copy(nmp[:, u % 2, 1, :], nms[:, 1, :]))
                nc.vector.tensor_tensor(nmp[:, u % 2, 2, :], nms[:, 1, :], nmp[:, u % 2, 1, :], ALU.subtract).then_inc(nmp_ready, 1)

            def head_outputs(u):
                b, quad = unit(u)
                dve.wait_ge(oqT_ps, u + 1)
                o = ps[:, M7, 0:S].rearrange("p (i k c) -> p i k c", i=2, c=32)
                link(nc.vector.reciprocal(rs2[:, 2 * b:2 * b + 2, 4 * quad:4 * quad + 4], o[:, :, :, HD2]))
                nc.vector.tensor_tensor(o2[:, 2 * b:2 * b + 2, 32 * quad:32 * quad + 32].rearrange("p i (k d) -> p i k d", d=HD2),
                                        o[:, :, :, 0:HD2],
                                        rs2[:, 2 * b:2 * b + 2, 4 * quad:4 * quad + 4].unsqueeze(3).to_broadcast([P, 2, 4, HD2]),
                                        ALU.mult).then_inc(o2_ready, 1)

            for i in range(UNITS + 3):
                if i < UNITS:
                    b, quad = unit(i)
                    for n in range(4 * i, 4 * i + 4):
                        qt, pair = 2 * b + n % 4 // 2, 2 * quad + n % 2
                        dve.wait_ge(s2_ps, n + 1)
                        nc.vector.tensor_reduce(m2[:, qt, 2 * pair:2 * pair + 2], ps[:, 2 * (n % 2):2 * (n % 2) + 2, :], AX.X, ALU.max).then_inc(m2_ready, 1)
                    split_max(i)
                if i >= 3:
                    head_outputs(i - 3)

            for t in range(NT):
                dve.wait_ge(y2_ps, t + 1)
                nc.vector.tensor_tensor(x2[:, t, :], ps[:, t, P:2 * P], x1[:, t, :], ALU.add).then_inc(x2_ready, 1)
            dve.wait_ge(x2_ready, NT)
            normalise(2, x2, range(NT), 4)

            dve.wait_ge(lg_ps, 1)
            br = xcol("br").unsqueeze(1).to_broadcast([P, NT, NE])
            link(nc.vector.tensor_tensor(lg[:, :, :], ps[:, M7, 0:NT * NE].rearrange("p (t e) -> p t e", e=NE), br, ALU.add))
            link(nc.vector.tensor_reduce(lmax[:, :], lg[:, :, :], AX.X, ALU.max))
            nc.vector.tensor_tensor(lg[:, :, :], lg[:, :, :], lmax[:, :].unsqueeze(2).to_broadcast([P, NT, NE]), ALU.subtract).then_inc(lg_ready, 1)
            dve.wait_ge(ex_ready, 1)
            link(nc.vector.tensor_reduce(esum[:, :], ex[:, :, :], AX.X, ALU.add))
            link(nc.vector.reciprocal(rsum[:, :], esum[:, :]))
            link(nc.vector.tensor_tensor(sc[:, :, :], ex[:, :, :], rsum[:, :].unsqueeze(2).to_broadcast([P, NT, NE]), ALU.mult))
            for t in range(NT):
                last = nc.vector.max(top[:, t, :], sc[:, t, :])
            link(last)
            for t in range(NT):
                last = nc.vector.max_index(topi[:, t, :], top[:, t, :], sc[:, t, :])
            link(last)
            link(nc.vector.tensor_copy(topf[:, :, :], topi[:, :, :]))
            iota = xcol("iota").unsqueeze(1).to_broadcast([P, NT, NE])
            for k in range(2):
                last = nc.vector.tensor_tensor(hit[:, k, :, :], iota, topf[:, :, k:k + 1].to_broadcast([P, NT, NE]), ALU.is_equal)
            link(last)
            for k in range(2):
                last = nc.vector.tensor_tensor(hw[:, k, :, :], hit[:, k, :, :], top[:, :, k:k + 1].to_broadcast([P, NT, NE]), ALU.mult)
            link(last)
            nc.vector.tensor_tensor(cw[:, :, :], hw[:, 0, :, :], hw[:, 1, :, :], ALU.add).then_inc(cw_ready, 1)
            dve.wait_ge(cwT_ps, 1)
            nc.vector.tensor_copy(cwT[:, :], ps[0:NE, M7, :]).then_inc(cwT_ready, 1)
            dve.wait_ge(db_ps, 1)
            nc.vector.tensor_tensor(acc[:, :, :], psb(6).rearrange("p (t d) -> p t d", t=NT), x2[:, :, :], ALU.add).then_inc(dn_used, 1)

            def combine(e):
                dve.wait_ge(dn_ps, e + 1)
                dve.wait_ge(dn_used, NT * e + 1)
                for t in range(NT):
                    nc.vector.scalar_tensor_tensor(acc[:, t, :], ps[:, 4 + e % 2, t * D:(t + 1) * D], cw[:, t, e:e + 1], acc[:, t, :],
                                                   ALU.mult, ALU.add).then_inc(acc_ready if e == NE - 1 else dn_used, 1)

            for n in range(NE * NC):
                e, c = n // NC, n % NC
                bias_g = w2[:, c2["gub"][0] + 4 * e + c:c2["gub"][0] + 4 * e + c + 1]
                dve.wait_ge(g_ps, n + 1)
                if n >= 2:
                    dve.wait_ge(glu_ready, n - 1)
                nc.vector.tensor_scalar(g1[:, n % 2, :], psb(n % 2), bias_g, 7.0, ALU.add, ALU.min).then_inc(g1_ready, 1)
                dve.wait_ge(u1_ready, n + 1)
                nc.vector.tensor_scalar(u2[:, n % 2, :], u1[:, n % 2, :], -7.0, 7.0, ALU.max, ALU.min).then_inc(u2_ready, 1)
                if c == 1 and e >= 1:
                    combine(e - 1)
                dve.wait_ge(u2_ready, n + 1)
                dve.wait_ge(glu_ready, n + 1)
                if e >= 2:
                    dve.wait_ge(dn_ps, e - 1)
                nc.vector.scalar_tensor_tensor(act_sb[:, e % 2, c, :], u2[:, n % 2, :], 1.0, glu[:, n % 2, :], ALU.add, ALU.mult).then_inc(act_ready, 1)
            combine(NE - 1)

        @block.tensor
        def _(pe):
            mm = nc.tensor.matmul

            pe.wait_ge(d_ctx, 16)
            pe.wait_ge(d_w2, 16)
            for c in range(2):
                last = mm(psb(2 + c), xcol("wk"), ctx_sb[:, c * 512:(c + 1) * 512], start=True, stop=True)
            last.then_inc(kv2_ps, 1)
            for k in range(B * NKT):
                last = mm(ps[:, 4 + k // 4, (k % 4) * P:(k % 4 + 1) * P], ctx_sb[:, k * P:(k + 1) * P], xcol("wv"), start=True, stop=True)
            last.then_inc(kv2_ps, 1)

            pe.wait_ge(d_w1, 16)
            for t in range(NT):
                pe.wait_ge(xn_ready, t + 1)
                last = nc.tensor.transpose(ps[:, O1, t * P:(t + 1) * P], xn[:, 0, t, :], identf)
            last.then_inc(xnT_ps, 1)
            pe.wait_ge(xnT_ready, 1)
            mm(psb(M7), wcol("wq"), xnT[:, 0, :], start=True, stop=True).then_inc(qkv1_ps, 1)
            mm(psb(0), wcol("wk"), xnT[:, 0, :], start=True, stop=True).then_inc(qkv1_ps, 1)
            for t in range(NT):
                mm(ps[:, 1, t * 32:(t + 1) * 32], xnT[:, 0, t * P:(t + 1) * P], wcol("wv"), start=True, stop=True)
            for b in range(B):
                k0 = b * S + P - WIN
                last = mm(ps[0:WIN, 1, 128 + b * 32:128 + (b + 1) * 32], xnT[:, 0, k0:k0 + WIN], wcol("wv"), start=True, stop=True)
            last.then_inc(qkv1_ps, 1)

            def strip_scores(t):
                k, a = t % 2, s1_bank(t)
                key0 = (t // 2) * S + (P - WIN if k else 0)
                if t >= 2:
                    pe.wait_ge(pT1a_ready, t - 1)
                    pe.wait_ge(pT1b_ready, t - 1)
                for i, (h0, h1) in enumerate(heads_of_bank(k)):
                    n = (h1 - h0) * STRIP[k]
                    mm(ps[:, a + i, 0:n], identb, mask_at[k][:, 0:n], start=True, stop=False)
                    last = mm(ps[:, a + i, 0:n].rearrange("p (h j) -> p h j", h=h1 - h0), qT[:, t * P:(t + 1) * P],
                              kexp[:, h0:h1, key0:key0 + STRIP[k]], start=False, stop=True)
                last.then_inc(s1_ps, 1)

            def strip_transposes(t):
                k, a = t % 2, s1_bank(t)
                pe.wait_ge(pn1_ready, t + 1)
                for h in range(H1):
                    last = nc.tensor.transpose(ps[:, a + h // 4, (h % 4) * P:(h % 4 + 1) * P], pn1[:, k, h, STRIP[k] - P:STRIP[k]], identf)
                last.then_inc(pT1_ps, 1)

            def strip_output(t):
                k = t % 2
                pe.wait_ge(pT1a_ready, t + 1)
                pe.wait_ge(pT1b_ready, t + 1)
                if t >= 1:
                    pe.wait_ge(x1_ready, t)
                if k == 1:
                    pe.wait_ge(spill_ready, t // 2 + 1)
                for h in range(H1):
                    last = mm(ps[:, O1, 0:P], vpad[:, t, h * P:(h + 1) * P], pT1[:, k, h, :], start=(h == 0), stop=(h == H1 - 1 and k == 0))
                if k == 1:
                    for h in range(H1):
                        last = mm(ps[:, O1, 0:WIN], vspill[:, t // 2, h * P:(h + 1) * P], pTs[:, h, :], start=False, stop=(h == H1 - 1))
                last.then_inc(o1_ps, 1)
                pe.wait_ge(oT1_ready, t + 1)
                mm(ps[:, O1, P:2 * P], oT1[:, k, :], wcol("wo"), start=True, stop=True).then_inc(y1_ps, 1)

            def queries2(b):
                for t in range(2 * b, 2 * b + 2):
                    pe.wait_ge(xn_ready, NT + t + 1)
                    if b == 1 and t == 2:
                        pe.wait_ge(qparts_ready, 1)
                    last = nc.tensor.transpose(ps[:, M7, (t % 2) * P:(t % 2 + 1) * P], xn[:, 1, t, :], identf)
                last.then_inc(xnT_ps, 1)
                pe.wait_ge(xnT_ready, 2 + b)
                mm(ps[:, M7, 0:S], xcol("wq"), xnT[:, 1, b * S:(b + 1) * S], start=True, stop=True).then_inc(q2_ps, 1)

            pe.wait_ge(d_msk, 16)
            pe.wait_ge(qT_ready, 1)
            pe.wait_ge(kexp_ready, H1)
            pe.wait_ge(vpad_ready, NT + B)
            pe.wait_ge(vaug_ready, 2)
            pe.wait_ge(kres_ready, 1)
            pe.wait_ge(xnT_ready, 1)
            strip_scores(0)
            strip_scores(1)
            strip_transposes(0)
            strip_output(0)
            strip_scores(2)
            strip_transposes(1)
            strip_output(1)
            strip_scores(3)
            queries2(0)
            strip_transposes(2)
            strip_output(2)
            strip_transposes(3)
            strip_output(3)
            queries2(1)

            pe.wait_ge(d_kst, 16 * H2)

            def row_scores(i, step):
                b, quad = unit(i)
                n = 4 * i + step
                qt, pair = step // 2, 2 * quad + step % 2
                if n >= 2:
                    pe.wait_ge(m2_ready, n - 1)
                else:
                    pe.wait_ge(pT1a_ready, NT)
                    pe.wait_ge(pT1b_ready, NT)
                for s in range(2):
                    last = mm(psb(2 * (n % 2) + s), qst[:, pair, b, s, qt * P:(qt + 1) * P], kst[:, pair, b * SK:(b + 1) * SK], start=True, stop=True)
                last.then_inc(s2_ps, 1)

            def max_rows(i):
                b, quad = unit(i)
                pe.wait_ge(m2_ready, 4 * (i + 1))
                if i >= 4:
                    pe.wait_ge(o2_ready, i - 3)
                elif i >= 1:
                    pe.wait_ge(nmp_ready, i)
                else:
                    pe.wait_ge(qparts_ready, 2 * 3)
                for j in range(2):
                    last = nc.tensor.transpose(ps[0:4, M7, j * P:(j + 1) * P], m2[:, 2 * b + j, 4 * quad:4 * quad + 4], identf)
                last.then_inc(mT_ps, 1)

            def key_scores(i, step):
                b, quad = unit(i)
                for pair in range(2):
                    n = 8 * i + 2 * step + pair
                    if n >= 2:
                        pe.wait_ge(p2_ready, n - 1)
                    k0 = b * SK + step * P
                    mm(psb(4 + n % 2), kst[:, 2 * quad + pair, k0:k0 + P], qst[:, 2 * quad + pair, b, :, :],
                       start=True, stop=True).then_inc(st_ps, 1)

            def weighted_values(i, step):
                b, quad = unit(i)
                if step == 0:
                    if i >= 1:
                        pe.wait_ge(oq_ready, i)
                    else:
                        pe.wait_ge(x1_ready, NT)
                pe.wait_ge(p2_ready, 8 * i + 2 * step + 2)
                for k in range(4):
                    last = mm(ps[32 * k:32 * k + 32, 6, 0:S], vaug[:, b * NKT + step, 4 * quad + k, :], pT2[:, i % 2, step, k, :],
                              start=(step == 0), stop=(step == NKT - 1))
                if step == NKT - 1:
                    last.then_inc(pv_ps, 1)

            def turn_outputs(i):
                pe.wait_ge(oq_ready, i + 1)
                pe.wait_ge(nmp_ready, min(i + 4, UNITS))
                if i >= 1:
                    pe.wait_ge(o2_ready, i)
                for j in range(2):
                    last = nc.tensor.transpose(ps[:, M7, j * P:(j + 1) * P], oq[:, i % 2, j * P:(j + 1) * P], identf)
                last.then_inc(oqT_ps, 1)

            for i in range(UNITS + 3):
                if i < UNITS and i % QUADS == 0:
                    pe.wait_ge(d_qst[i // QUADS], 16 * H2)
                if 2 <= i < UNITS + 2:
                    pe.wait_ge(d_nm[i - 2], 16 * 4)
                for step in range(4):
                    if i < UNITS:
                        row_scores(i, step)
                    if 2 <= i < UNITS + 2:
                        key_scores(i - 2, step)
                    if i >= 3:
                        weighted_values(i - 3, step)
                if i < UNITS:
                    max_rows(i)
                if i >= 3:
                    turn_outputs(i - 3)

            pe.wait_ge(o2_ready, UNITS)
            for t in range(NT):
                nc.tensor.transpose(ps[:, t, 0:P], o2[:, t, :], identf).then_inc(o2T_ps, 1)
            for t in range(NT):
                pe.wait_ge(o2T_ready, t + 1)
                mm(ps[:, t, P:2 * P], o2T[:, t, :], xcol("wo"), start=True, stop=True).then_inc(y2_ps, 1)
            for t in range(NT):
                pe.wait_ge(xn_ready, 2 * NT + t + 1)
                last = nc.tensor.transpose(ps[:, 4, t * P:(t + 1) * P], xn[:, 2, t, :], identf)
            last.then_inc(xnT_ps, 1)
            pe.wait_ge(xnT_ready, 4)
            for t in range(NT):
                last = mm(ps[:, M7, t * NE:(t + 1) * NE], xnT[:, 2, t * P:(t + 1) * P], xcol("wr"), start=True, stop=True)
            last.then_inc(lg_ps, 1)

            def up(e):
                for c in range(NC):
                    n = e * NC + c
                    if n >= 2:
                        pe.wait_ge(g1_ready, n - 1)
                    mm(psb(n % 2), gu_sb[:, e, c * P:(c + 1) * P], xnT[:, 2, :], start=True, stop=True).then_inc(g_ps, 1)
                    if n >= 2:
                        pe.wait_ge(u1_ready, n - 1)
                    mm(psb(2 + n % 2), gu_sb[:, e, FI + c * P:FI + (c + 1) * P], xnT[:, 2, :], start=True, stop=True).then_inc(u_ps, 1)

            def down(e):
                pe.wait_ge(act_ready, NC * (e + 1))
                if e >= 2:
                    pe.wait_ge(dn_used, 1 + NT * (e - 1))
                for t in range(NT):
                    for c in range(NC):
                        last = mm(ps[:, 4 + e % 2, t * D:(t + 1) * D], act_sb[:, e % 2, c, t * P:(t + 1) * P], dn_sb[:, e, c, :],
                                  start=(c == 0), stop=(c == NC - 1))
                last.then_inc(dn_ps, 1)

            pe.wait_ge(d_gu, 16)
            pe.wait_ge(d_dn, 32)
            up(0)
            pe.wait_ge(cw_ready, 1)
            for t in range(NT):
                last = nc.tensor.transpose(ps[0:NE, M7, t * P:(t + 1) * P], cw[:, t, :], identf)
            last.then_inc(cwT_ps, 1)
            pe.wait_ge(cwT_ready, 1)
            for t in range(NT):
                last = mm(ps[:, 6, t * D:(t + 1) * D], cwT[:, t * P:(t + 1) * P], db_sb[:, :], start=True, stop=True)
            last.then_inc(db_ps, 1)
            for e in range(1, NE):
                up(e)
                down(e - 1)
            down(NE - 1)


def kernel(**inputs):
    import ml_dtypes
    import concourse.bacc as bacc
    from concourse.bass_utils import run_bass_kernel_spmd

    a = {k: np.asarray(v) for k, v in inputs.items()}
    f32 = np.float32
    rows = lambda v: np.broadcast_to(v.reshape(1, -1), (P, v.size))
    heads = np.zeros((P, H1), f32)
    for h in range(H1):
        heads[h * HD1:(h + 1) * HD1, h] = 1
    rep = lambda w: np.repeat(w.reshape(KV, 1, HD1, -1), H1 // KV, axis=1).reshape(P, -1)
    pack1 = dict(wq=a["L0_attn_Wq"].T, wk=rep(a["L0_attn_Wk"]).T, wv=a["L0_attn_Wv"].T, wo=a["L0_attn_Wo"].T,
                 ident=np.eye(P, dtype=f32), bq=a["L0_attn_bq"].reshape(P, 1), bk=rep(a["L0_attn_bk"]),
                 sink=rows(a["L0_attn_sink_bias"]), bv=rows(a["L0_attn_bv"]), bo=rows(a["L0_attn_bo"]), head=heads)
    pack2 = dict(wq=a["L0_xattn_Wq"].T, wk=a["L0_xattn_Wk"].T, wv=a["L0_xattn_Wv"].T, wo=a["L0_xattn_Wo"].T,
                 wr=a["L0_ffn_router_weight"].T, br=rows(a["L0_ffn_router_bias"]),
                 gub=a["L0_ffn_gate_up_bias"].reshape(4 * NE, P).T, iota=rows(np.arange(NE, dtype=f32)))
    q, j = np.arange(P)[:, None], np.arange(STRIP[1])[None, :]
    first = (j[:, :P] <= q) & (j[:, :P] > q - WIN)
    second = (j - WIN <= q) & (j > q)
    masks = [np.tile(np.where(ok, 0.0, MASKED), (1, n)) for ok, n in ((first, HB[0]), (second, HB[1]))]
    maskc = np.concatenate(masks + [np.eye(P)], axis=1).astype(ml_dtypes.bfloat16)
    arrays = dict(
        x=a["x"].reshape(T, D), ctxT=a["ctx_1024"].reshape(B * SK, D).T,
        pack1=np.concatenate([pack1[k] for k in PACK1], axis=1), pack2=np.concatenate([pack2[k] for k in PACK2], axis=1),
        maskc=maskc, gu=a["L0_ffn_gate_up_proj"], dn=a["L0_ffn_down_proj"], db=a["L0_ffn_down_bias"])
    arrays = {k: np.ascontiguousarray(v) for k, v in arrays.items()}

    nc = bacc.Bacc("TRN2", target_bir_lowering=False, num_devices=1)
    args = [nc.dram_tensor(k, v.shape, mybir.dt.from_np(v.dtype), kind="ExternalInput").ap() for k, v in arrays.items()]
    out = nc.dram_tensor("out", (T, D), mybir.dt.float32, kind="ExternalOutput").ap()
    build(nc, *args, out)
    r = run_bass_kernel_spmd(nc, [arrays], core_ids=[0])
    return r.results[0]["out"].reshape(B, S, D)
```

```python
import numpy as np
import concourse.bass as bass
from concourse import mybir
from contextlib import ExitStack

P = 128
B, S, D = 2, 256, 128
T = B * S
NT = T // P
SK = 512
NKT = SK // P
H1, KV, HD1, WIN = 8, 2, 16, 32
H2, HD2 = 16, 8
NE, FI = 8, 256
NC = FI // P
TERMS = 6
STACK = 64
NM_ROW = HD2 * TERMS
NPAIR = H2 // 2
QUADS = 4
UNITS = B * QUADS
STEPS = 4 * UNITS
LAG2 = 8
LAGV = 2
RING = 4
LAST = STEPS + LAG2 + LAGV + 1
NX = B * NE
AHEAD = 4
FFN_FROM = STEPS
EPS = 1e-5
ONES2 = float(np.uint32(0x3F803F80).view(np.float32))
MASKED = -1e30
STRIP = (P, P + WIN)
HB = (4, 3)
VC = 2 * HD1
Q_PARTS = (0, 0, 0, 1, 1, 2)
K_PARTS = (0, 1, 2, 0, 1, 0)

PACK1 = dict(ident=P, wq=P, wk=P, wv=P, bq=1, bk=1, sink=1, head=H1, wo=P, bv=P, bo=D)
PACK2 = dict(wq=P, wk=P, wv=P, wo=P, wr=NE, br=NE, gub=4 * NE, iota=NE)


def columns(pack):
    at, out = 0, {}
    for name, n in pack.items():
        out[name] = (at, at + n)
        at += n
    return out, at


def build(nc, x, ctxT, pack1, pack2, maskc, gu, dn, db, out):
    fp32, bf16, u32 = mybir.dt.float32, mybir.dt.bfloat16, mybir.dt.uint32
    ALU, ACT, AX = mybir.AluOpType, mybir.ActivationFunctionType, mybir.AxisListType
    c1, n1 = columns(PACK1)
    c2, n2 = columns(PACK2)

    with ExitStack() as ctx:
        def sb(name, shape, dt=fp32):
            return ctx.enter_context(nc.sbuf_tensor(name, shape, dt))

        def sem(name):
            return ctx.enter_context(nc.semaphore(name))

        xs = sb("xs", [P, NT, D])
        xbo = sb("xbo", [P, NT, D])
        w1 = sb("w1", [P, n1])
        w2 = sb("w2", [P, n2])
        msk = sb("msk", [P, 4 * P + 3 * STRIP[1] + P], bf16)
        ctx_sb = sb("ctx_sb", [P, B * SK])
        db_sb = sb("db_sb", [NE, D])
        stats = sb("stats", [P, 3, NT, 6])
        mv = sb("mv", [P, 3, NT, 2])
        veps = sb("veps", [P, 3, NT])
        mhalf = sb("mhalf", [P, NT])
        rstd = sb("rstd", [P, 3, NT])
        xn = sb("xn", [P, 3, NT, D])
        xnT = sb("xnT", [P, 3, T])
        qT = sb("qT", [P, T])
        kT = sb("kT", [P, T])
        vpad = sb("vpad", [P, NT, H1, VC])
        vspill = sb("vspill", [WIN, B, H1, VC])
        negm1 = sb("negm1", [P, NT, H1])
        rmax1 = sb("rmax1", [P, NT, H1])
        sums1 = sb("sums1", [P, NT, H1])
        esink = sb("esink", [P, NT, H1])
        den1 = sb("den1", [P, NT, H1])
        rden1 = sb("rden1", [P, NT, H1])
        pT1 = sb("pT1", [P, 2, H1, P])
        pTs = sb("pTs", [WIN, H1, WIN])
        oT1 = sb("oT1", [P, 2, P])
        x1 = sb("x1", [P, NT, D])
        kparts = sb("kparts", [P, TERMS, B * SK], bf16)
        kres = sb("kres", [P, B * SK])
        qparts = sb("qparts", [P, TERMS, T], bf16)
        qres = sb("qres", [P, T])
        kst = sb("kst", [P, NPAIR, B * SK], bf16)
        qst = sb("qst", [P, NPAIR, B, 2, S], bf16)
        vaug = sb("vaug", [P, B * NKT, H2, 32])
        m2 = sb("m2", [P, NT, H2])
        nmr = sb("nmr", [P, 2, 2, 2, 2])
        nmq = sb("nmq", [P, 2, 2, 2, 3, 2], bf16)
        nmp = sb("nmp", [12, 2, S], bf16)
        pT2 = sb("pT2", [P, RING, 4, S])
        pn1 = pT2[:, :, :, :].rearrange("p a b c -> p (a b c)")[:, 0:2 * H1 * STRIP[1]].rearrange("p (n h j) -> p n h j", n=2, h=H1)
        big = sb("big", [P, 14 * T])
        oq = sb("oq", [P, 2, S])
        rs2 = sb("rs2", [P, NT, H2])
        o2 = xs
        o2T = sb("o2T", [P, T])
        x2 = sb("x2", [P, NT, D])
        lg = sb("lg", [P, NT, NE])
        lmax = sb("lmax", [P, NT])
        ex = sb("ex", [P, NT, NE])
        esum = sb("esum", [P, NT])
        rsum = sb("rsum", [P, NT])
        sc = sb("sc", [P, NT, NE])
        top = sb("top", [P, NT, 8])
        topi = sb("topi", [P, NT, 8], u32)
        topf = sb("topf", [P, NT, 8])
        hit = sb("hit", [P, 2, NT, NE])
        hw = sb("hw", [P, 2, NT, NE])
        cw = sb("cw", [P, NT, NE])
        cwT = sb("cwT", [NE, T])
        cwh = sb("cwh", [P, NT, NE])
        bup = sb("bup", [P, 4 * NE])
        spare = big
        g1, th, u1, u3, gu3 = (spare[:, 2 * S * k:2 * S * (k + 1)].rearrange("p (n t) -> p n t", n=2) for k in range(5))
        act_sb = spare[:, 10 * S:10 * S + AHEAD * NC * S].rearrange("p (n c t) -> p n c t", n=AHEAD, c=NC)
        kexp = spare[:, 0:H1 * T].rearrange("p (h t) -> p h t", h=H1)
        p1 = spare[:, H1 * T:H1 * T + 2 * H1 * STRIP[1]].rearrange("p (n h j) -> p n h j", n=2, h=H1)
        wexp = sb("wexp", [P, NE * 2 * FI + NE * NC * D])
        gu_sb = wexp[:, 0:NE * 2 * FI].rearrange("p (e n) -> p e n", e=NE)
        dn_sb = wexp[:, NE * 2 * FI:].rearrange("p (e c d) -> p e c d", e=NE, c=NC)
        acc = xbo

        wcol = lambda name: w1[:, c1[name][0]:c1[name][1]]
        xcol = lambda name: w2[:, c2[name][0]:c2[name][1]]
        identf = wcol("ident")
        mask_at = (msk[:, 0:4 * P], msk[:, 4 * P:4 * P + 3 * STRIP[1]])
        identb = msk[:, 4 * P + 3 * STRIP[1]:]

        ps = ctx.enter_context(nc.psum_tensor("ps", [P, 8, 512], fp32))
        psb = lambda b: ps[:, b, :]

        d_x, d_w1, d_msk, d_ctx, d_w2, d_gu, d_dn = (sem(n) for n in
                                                     ("d_x", "d_w1", "d_msk", "d_ctx", "d_w2", "d_gu", "d_dn"))
        d_kst = [sem(f"d_kst{u}") for u in range(QUADS)]
        d_qst = [sem(f"d_qst{u}") for u in range(UNITS)]
        d_nm = [sem(f"d_nm{u}") for u in range(UNITS)]
        d_out = sem("d_out")
        zeroed = sem("zeroed")
        vzeroed = sem("vzeroed")
        chain = sem("chain")
        kmid_ready = sem("kmid_ready")
        var_ready, rstd_ready, xn_ready, xbo_ready = sem("var_ready"), sem("rstd_ready"), sem("xn_ready"), sem("xbo_ready")
        xnT_ps, xnT_ready = sem("xnT_ps"), sem("xnT_ready")
        kv2_ps = sem("kv2_ps")
        khi_ready, kres_ready, kparts_ready, vaug_ready = (sem("khi_ready"), sem("kres_ready"), sem("kparts_ready"), sem("vaug_ready"))
        qkv1_ps = sem("qkv1_ps")
        qT_ready, kT_ready, kexp_ready, vpad_ready = sem("qT_ready"), sem("kT_ready"), sem("kexp_ready"), sem("vpad_ready")
        s1_ps, negm1_ready, p1_ready, esink_ready, pn1_ready = (sem("s1_ps"), sem("negm1_ready"), sem("p1_ready"), sem("esink_ready"), sem("pn1_ready"))
        spill_ready = sem("spill_ready")
        pT1_ps, pT1a_ready, pT1b_ready = sem("pT1_ps"), sem("pT1a_ready"), sem("pT1b_ready")
        q2_ps, qhi_ready, qres_ready, qparts_ready = sem("q2_ps"), sem("qhi_ready"), sem("qres_ready"), sem("qparts_ready")
        s2_ps, m2_ready = sem("s2_ps"), sem("m2_ready")
        gu3_ready, th_ready, u3_ready, bup_ready = sem("gu3_ready"), sem("th_ready"), sem("u3_ready"), sem("bup_ready")
        nmq_ready = sem("nmq_ready")
        m7_full, m7_read = sem("m7_full"), sem("m7_read")
        st_ps, p2_ready = sem("st_ps"), sem("p2_ready")
        pv_step, oq_ready, oqT_ps, o2_ready = sem("pv_step"), sem("oq_ready"), sem("oqT_ps"), sem("o2_ready")
        lg_ps, lg_ready, ex_ready, cw_ready = sem("lg_ps"), sem("lg_ready"), sem("ex_ready"), sem("cw_ready")
        cwT_ps, cwT_ready, db_ps, acc_ready = sem("cwT_ps"), sem("cwT_ready"), sem("db_ps"), sem("acc_ready")
        g_ps, u_ps, g1_ready, sg_ready, u1_ready = sem("g_ps"), sem("u_ps"), sem("g1_ready"), sem("sg_ready"), sem("u1_ready")
        u2_ready, glu_ready, act_ready, dn_ps, dn_used = (sem("u2_ready"), sem("glu_ready"), sem("act_ready"), sem("dn_ps"), sem("dn_used"))

        block = ctx.enter_context(nc.Block())
        turned_at = lambda g: (g - LAG2 - LAGV - 4) // 4 if g >= LAG2 + LAGV + 4 and (g - LAG2 - LAGV) % 4 == 0 else None

        def uses_at(g):
            out = [("o1", 3), ("y1", 3)] if g == 0 else []
            if g % 4 == 0 and 4 <= g < STEPS + 4:
                out.append(("maxima", g // 4 - 1))
            if turned_at(g) is not None:
                out.append(("outputs", turned_at(g)))
            return out + [u for at, u in ((3, ("xn2", 1)), (5, ("q2", 1)), (27, ("o2T", 0)), (29, ("y2", 0)), (31, ("xn3", 0)),
                                          (33, ("router", 0)), (35, ("cwT", 0)), (37, ("bias", 0))) if at == g]

        LATE = {4: [("o2T", 1), ("y2", 1)], 5: [("xn3", 1)], 6: [("router", 1)], 7: [("cwT", 1)], 8: [("bias", 1)]}
        USES = [("q1", 0), ("o1", 0), ("y1", 0), ("o1", 1), ("y1", 1), ("xn2", 0), ("q2", 0), ("o1", 2), ("y1", 2)] + [u for g in range(LAST + 1) for u in uses_at(g)] + [u for m in sorted(LATE) for u in LATE[m]]
        use = {u: k for k, u in enumerate(USES)}
        heads_of_bank = lambda k: [(i, min(i + HB[k], H1)) for i in range(0, H1, HB[k])]
        s1_bank = lambda t: (0, 2, 5, 2)[t]
        M7 = 7
        unit = lambda u: (u // QUADS, u % QUADS)

        @block.sync
        def _(sp):
            sp.dma_start(xs[:, :, :], x.rearrange("(t p) d -> p t d", p=P)).then_inc(d_x, 16)
            sp.dma_start(w1[:, :], pack1).then_inc(d_w1, 16)
            sp.dma_start(msk[:, :], maskc).then_inc(d_msk, 16)
            sp.dma_start(gu_sb[:, :, :], gu.rearrange("e p n -> p e n")).then_inc(d_gu, 16)
            sp.dma_start(dn_sb[:, :, :, :], dn.rearrange("e (c p) d -> p e c d", p=P)).then_inc(d_dn, 16)
            sp.dma_start(db_sb[:, :], db).then_inc(d_dn, 16)
            sp.wait_ge(khi_ready, 2)
            sp.wait_ge(kmid_ready, 1)
            sp.wait_ge(kparts_ready, 4)
            sp.wait_ge(zeroed, 5)
            for h in range(H2):
                r = STACK * (h % 2)
                sp.dma_start(kst[r:r + NM_ROW, h // 2, :], kparts[h * HD2:(h + 1) * HD2, :, :]).then_inc(d_kst[h // 4], 16)
            def stack_queries(b, heads):
                sp.wait_ge(qparts_ready, 2 * (b + 1))
                sp.wait_ge(m7_read, use["q2", b] + 1)
                for h in heads:
                    r = STACK * (h % 2)
                    sp.dma_start(qst[r:r + NM_ROW, h // 2, b, h % 2, :],
                                 qparts[h * HD2:(h + 1) * HD2, :, b * S:(b + 1) * S]).then_inc(d_qst[b * QUADS + h // 4], 16)

            def stack_maxima(u):
                b, quad = unit(u)
                sp.wait_ge(m7_read, use["maxima", u] + 1)
                for s in range(2):
                    r = STACK * s + NM_ROW
                    sp.dma_start(qst[r:r + 3, 2 * quad:2 * quad + 2, b, s, :], nmp[6 * s:6 * s + 6, u % 2, :]).then_inc(d_nm[u], 16)

            stack_queries(0, range(H2))
            stack_maxima(0)
            stack_queries(1, range(0, 8))
            stack_maxima(1)
            stack_queries(1, range(8, H2))
            for u in range(2, UNITS):
                stack_maxima(u)
            for b in range(B):
                sp.wait_ge(acc_ready, 2 * (b + 1))
                sp.dma_start(out[b * S:(b + 1) * S, :].rearrange("(t p) d -> p t d", p=P), acc[:, 2 * b:2 * b + 2, :]).then_inc(d_out, 16)
            sp.wait_ge(d_out, 16 * B)

        def gate_times_up(pool, m):
            for n in range(NC * m, NC * (m + 1)):
                pool.wait_ge(g1_ready, n + 1)
                pool.wait_ge(u3_ready, n + 1)
                if n >= 2:
                    pool.wait_ge(act_ready, n - 1)
                nc.gpsimd.tensor_tensor(gu3[:, n % 2, :], g1[:, n % 2, :], u3[:, n % 2, :], ALU.mult).then_inc(gu3_ready, 1)

        @block.gpsimd
        def _(pool):
            nc.gpsimd.memset(mhalf[:, :], -0.5).then_inc(zeroed, 1)
            nc.gpsimd.memset(vaug[:, :, :, :], 0.0).then_inc(zeroed, 1)
            pool.wait_ge(var_ready, 1)
            pool.wait_ge(zeroed, 2)
            nc.gpsimd.tensor_tensor(rstd[:, 0, :], veps[:, 0, :], mhalf[:, :], ALU.pow).then_inc(rstd_ready, 1)
            nc.gpsimd.memset(vaug[:, :, :, HD2:HD2 + 1], 1.0).then_inc(zeroed, 1)
            nc.gpsimd.memset(kst[:, :, :].bitcast(fp32), ONES2).then_inc(zeroed, 1)
            nc.gpsimd.memset(qst[:, :, :, :, :].rearrange("p a b c d -> p (a b c d)").bitcast(fp32), 0.0).then_inc(zeroed, 1)
            pool.wait_ge(d_x, 16)
            pool.wait_ge(d_w1, 16)
            nc.gpsimd.tensor_tensor(xbo[:, :, :], xs[:, :, :], wcol("bo").unsqueeze(1).to_broadcast([P, NT, D]), ALU.add).then_inc(xbo_ready, 1)
            pool.wait_ge(kres_ready, 1)
            nc.gpsimd.tensor_copy(kparts[:, 1, :], kres[:, :]).then_inc(kmid_ready, 1)
            nc.gpsimd.tensor_copy(kparts[:, 4, :], kres[:, :]).then_inc(kparts_ready, 1)
            pool.wait_ge(kmid_ready, 1)
            nc.gpsimd.tensor_tensor(kparts[:, 2, :], kres[:, :], kparts[:, 1, :], ALU.subtract).then_inc(kparts_ready, 1)
            pool.wait_ge(d_w2, 16)
            nc.gpsimd.tensor_scalar(bup[:, :], xcol("gub"), 1.0, None, ALU.add).then_inc(bup_ready, 1)
            for k, (n, b) in enumerate(((1, 0), (1, 1), (2, 0), (2, 1))):
                if k == 3:
                    for m in range(AHEAD + 1):
                        gate_times_up(pool, m)
                pool.wait_ge(var_ready, 2 + k)
                nc.gpsimd.tensor_tensor(rstd[:, n, 2 * b:2 * b + 2], veps[:, n, 2 * b:2 * b + 2], mhalf[:, 0:2], ALU.pow).then_inc(rstd_ready, 1)
            for m in range(AHEAD + 1, NX):
                gate_times_up(pool, m)

        @block.scalar
        def _(act):
            act.dma_start(ctx_sb[:, :], ctxT).then_inc(d_ctx, 16)
            act.dma_start(w2[:, :], pack2).then_inc(d_w2, 16)
            act.wait_ge(xnT_ps, 1)
            nc.scalar.activation(xnT[:, 0, :], psb(6), ACT.Copy).then_inc(xnT_ready, 1)
            act.wait_ge(qkv1_ps, 1)
            nc.scalar.activation(kT[:, :], psb(0), ACT.Identity, bias=wcol("bk")).then_inc(kT_ready, 1)
            def context_keys():
                act.wait_ge(kv2_ps, 1)
                for c in range(2):
                    nc.scalar.activation(kparts[:, 0, c * 512:(c + 1) * 512], psb(5 + c), ACT.Copy).then_inc(khi_ready, 1)

            def context_values():
                act.wait_ge(khi_ready, 2)
                for j, term in enumerate((3, 5)):
                    nc.scalar.activation(kparts[:, term, :], kparts[:, 0, :], ACT.Copy).then_inc(kparts_ready, 1)
                act.wait_ge(kv2_ps, 2)
                act.wait_ge(zeroed, 3)
                for c in range(2):
                    nc.scalar.activation(vaug[:, 4 * c:4 * c + 4, :, 0:HD2],
                                         psb(5 + c).rearrange("p (t h d) -> p t h d", t=4, d=HD2), ACT.Copy).then_inc(vaug_ready, 1)

            def softmax1(t):
                k = t % 2
                act.wait_ge(negm1_ready, t + 1)
                for i, (h0, h1) in enumerate(heads_of_bank(k)):
                    for h in range(h0, h1):
                        src = ps[:, s1_bank(t) + i, (h - h0) * STRIP[k]:(h - h0 + 1) * STRIP[k]]
                        if t >= 2 and h == 0:
                            act.wait_ge(pn1_ready, t - 1)
                        nc.scalar.activation(p1[:, k, h, 0:STRIP[k]], src, ACT.Exp, bias=negm1[:, t, h:h + 1],
                                             accum_out=sums1[:, t, h:h + 1]).then_inc(p1_ready, 1)
                nc.scalar.activation(esink[:, t, :], negm1[:, t, :], ACT.Exp, bias=wcol("sink")).then_inc(esink_ready, 1)

            def pT1_half(t):
                act.wait_ge(pT1_ps, t + 1)
                if t >= 2:
                    act.wait_ge(m7_full, use["o1", t - 2] + 1)
                nc.scalar.activation(pT1[:, t % 2, 0:4, :], psb(s1_bank(t)).rearrange("p (h q) -> p h q", h=4), ACT.Copy).then_inc(pT1a_ready, 1)

            def turn1(t):
                act.wait_ge(m7_full, use["o1", t] + 1)
                nc.scalar.activation(oT1[:, t % 2, :], ps[:, M7, 0:P], ACT.Copy).then_inc(m7_read, 1)

            def single(kind, b):
                k = use[kind, b]
                cols = slice(b * S, (b + 1) * S)
                if kind in ("xn2", "o2T", "xn3"):
                    dst = {"xn2": xnT[:, 1, cols], "o2T": o2T[:, cols], "xn3": xnT[:, 2, cols]}[kind]
                    act.wait_ge(m7_full, k + 1)
                    nc.scalar.activation(dst, ps[:, M7, 0:S], ACT.Copy).then_inc(m7_read, 1)
                if kind == "q2":
                    act.wait_ge(m7_full, k + 1)
                    nc.scalar.activation(qparts[:, 0:3, cols], ps[:, M7, 0:S].unsqueeze(1).to_broadcast([P, 3, S]), ACT.Copy).then_inc(qhi_ready, 1)
                if kind == "router":
                    act.wait_ge(lg_ready, b + 1)
                    nc.scalar.activation(ex[:, 2 * b:2 * b + 2, :], lg[:, 2 * b:2 * b + 2, :], ACT.Exp).then_inc(ex_ready, 1)

            softmax1(0)
            context_keys()
            softmax1(1)
            pT1_half(0)
            turn1(0)
            context_values()
            pT1_half(1)
            turn1(1)
            softmax1(2)
            single("xn2", 0)
            single("q2", 0)
            pT1_half(2)
            turn1(2)
            softmax1(3)

            def exponentials(g):
                if g >= RING:
                    act.wait_ge(pv_step, g - RING + 1)
                for pair in range(2):
                    n = 2 * g + pair
                    act.wait_ge(st_ps, n + 1)
                    nc.scalar.activation(pT2[:, g % RING, 2 * pair:2 * pair + 2, :],
                                         psb(4 + n % 2).rearrange("p (s q) -> p s q", s=2), ACT.Exp,
                                         scale=float(HD2) ** -0.5).then_inc(p2_ready, 1)

            def out_quad(u):
                act.wait_ge(pv_step, 4 * u + 4)
                if u >= 2:
                    act.wait_ge(m7_full, use["outputs", u - 2] + 1)
                nc.scalar.activation(oq[:, u % 2, :], ps[:, 6, 0:S], ACT.Copy).then_inc(oq_ready, 1)

            def expert_half(n):
                bias_u = bup[:, 4 * (n // NC % NE) + NC + n % NC:4 * (n // NC % NE) + NC + n % NC + 1]
                act.wait_ge(u_ps, n + 1)
                if n == 0:
                    act.wait_ge(bup_ready, 1)
                if n >= 2:
                    act.wait_ge(u3_ready, n - 1)
                nc.scalar.activation(u1[:, n % 2, :], ps[:, 2 + n % 2, 0:S], ACT.Identity, bias=bias_u).then_inc(u1_ready, 1)
                act.wait_ge(g1_ready, n + 1)
                if n >= 2:
                    act.wait_ge(act_ready, n - 1)
                nc.scalar.activation(th[:, n % 2, :], g1[:, n % 2, :], ACT.Tanh, scale=0.5 * 1.702).then_inc(th_ready, 1)

            for g in range(LAST + 1):
                if LAG2 <= g < STEPS + LAG2:
                    exponentials(g - LAG2)
                if g == 0:
                    pT1_half(3)
                    turn1(3)
                if g >= LAG2 + LAGV and (g - LAG2 - LAGV) % 4 == 3:
                    out_quad((g - LAG2 - LAGV) // 4)
                for kind, k in uses_at(g):
                    if kind not in ("maxima", "outputs", "o1", "y1"):
                        single(kind, k)
                if FFN_FROM <= g < FFN_FROM + NC * AHEAD:
                    expert_half(g - FFN_FROM)
            for m in range(AHEAD, NX):
                late = LATE.get(m, [])
                if ("o2T", 1) in late:
                    single("o2T", 1)
                for n in range(NC * m, NC * (m + 1)):
                    expert_half(n)
                for kind, b in late:
                    if kind != "o2T":
                        single(kind, b)

        @block.vector
        def _(dve):
            links = [0]

            def link(ins):
                links[0] += 1
                ins.then_inc(chain, 1)
                dve.wait_ge(chain, links[0])

            def moments(n, src, tiles):
                for t in tiles:
                    links[0] += 1
                    nc.vector.bn_stats(stats[:, n, t, :], src[:, t, :]).then_inc(chain, 1)
                dve.wait_ge(chain, links[0])
                for t in tiles:
                    last = nc.vector.bn_aggr(mv[:, n, t, :], stats[:, n, t, :])
                link(last)
                tt = slice(tiles[0], tiles[-1] + 1)
                nc.vector.tensor_scalar(veps[:, n, tt], mv[:, n, tt, 1], EPS, None, ALU.add).then_inc(var_ready, 1)

            def normalise(n, src, tiles, k):
                dve.wait_ge(rstd_ready, k)
                for t in tiles:
                    nc.vector.tensor_scalar(xn[:, n, t, :], src[:, t, :], mv[:, n, t, 0:1], rstd[:, n, t:t + 1],
                                            ALU.subtract, ALU.mult).then_inc(xn_ready, 1)

            tiles_of = lambda b: range(2 * b, 2 * b + 2)

            nc.vector.memset(vpad[:, :, :, :], 0.0).then_inc(vzeroed, 1)
            nc.vector.memset(vspill[:, :, :, :], 0.0).then_inc(vzeroed, 1)
            dve.wait_ge(d_x, 16)
            moments(0, xs, range(NT))
            normalise(0, xs, range(NT), 1)

            dve.wait_ge(d_w1, 16)
            dve.wait_ge(m7_full, use["q1", 0] + 1)
            nc.vector.tensor_scalar(qT[:, :], psb(M7), wcol("bq"), float(HD1) ** -0.5, ALU.add, ALU.mult).then_inc(m7_read, 1)
            dve.wait_ge(kT_ready, 1)
            def spread_keys(b):
                cols = slice(b * S, (b + 1) * S)
                for h in range(H1):
                    nc.vector.tensor_scalar(kexp[:, h, cols], kT[:, cols], w1[:, c1["head"][0] + h:c1["head"][0] + h + 1], None, ALU.mult).then_inc(kexp_ready, 1)

            by_pair = lambda v: v.rearrange("p h c -> p (h c)").rearrange("p (g k d) -> p g k d", k=4, d=HD1)[:, :, 0:4:3, :]
            rows = lambda v: v.rearrange("p (g r d) -> p g r d", r=2, d=HD1)
            spread_keys(0)
            dve.wait_ge(qkv1_ps, 2)
            dve.wait_ge(vzeroed, 2)
            for b in range(B):
                nc.vector.tensor_tensor(by_pair(vspill[:, b, :, :]), rows(ps[0:WIN, 2, b * P:(b + 1) * P]), rows(wcol("bv")[0:WIN]), ALU.add).then_inc(vpad_ready, 1)
            for t in range(NT):
                nc.vector.tensor_tensor(by_pair(vpad[:, t, :, :]), rows(ps[:, 5, t * P:(t + 1) * P]), rows(wcol("bv")), ALU.add).then_inc(vpad_ready, 1)

            def context_keys():
                dve.wait_ge(khi_ready, 2)
                link(nc.vector.tensor_tensor(kres[:, 0:512], psb(5), kparts[:, 0, 0:512], ALU.subtract))
                nc.vector.tensor_tensor(kres[:, 512:1024], psb(6), kparts[:, 0, 512:1024], ALU.subtract).then_inc(kres_ready, 1)

            def maxima1(t):
                k = t % 2
                dve.wait_ge(s1_ps, t + 1)
                if k == 0:
                    link(nc.vector.tensor_reduce(rmax1[:, t, :], ps[:, s1_bank(t):s1_bank(t) + 2, :].rearrange("p b (h j) -> p (b h) j", h=4), AX.X, ALU.max))
                else:
                    a = s1_bank(t)
                    nc.vector.tensor_reduce(rmax1[:, t, 0:6].rearrange("p (b h) -> p b h", b=2),
                                            ps[:, a:a + 2, 0:3 * STRIP[1]].rearrange("p b (h j) -> p b h j", h=3), AX.X, ALU.max)
                    link(nc.vector.tensor_reduce(rmax1[:, t, 6:8], ps[:, a + 2, 0:2 * STRIP[1]].rearrange("p (h j) -> p h j", h=2), AX.X, ALU.max))
                nc.vector.tensor_scalar(negm1[:, t, :], rmax1[:, t, :], wcol("sink"), -1.0, ALU.max, ALU.mult).then_inc(negm1_ready, 1)

            def normalise_p(t):
                k = t % 2
                dve.wait_ge(p1_ready, H1 * (t + 1))
                dve.wait_ge(esink_ready, t + 1)
                link(nc.vector.tensor_tensor(den1[:, t, :], sums1[:, t, :], esink[:, t, :], ALU.add))
                link(nc.vector.reciprocal(rden1[:, t, :], den1[:, t, :]))
                if t >= 2:
                    dve.wait_ge(pT1_ps, t - 1)
                nc.vector.tensor_tensor(pn1[:, k, :, 0:STRIP[k]], p1[:, k, :, 0:STRIP[k]],
                                        rden1[:, t, :].unsqueeze(2).to_broadcast([P, H1, STRIP[k]]), ALU.mult).then_inc(pn1_ready, 1)
                if k == 1:
                    dve.wait_ge(pn1_ready, t + 1)
                    if t == 3:
                        dve.wait_ge(m7_full, use["o1", 1] + 1)
                    nc.vector.transpose(pTs[:, :, :], pn1[0:WIN, 1, :, 0:WIN]).then_inc(spill_ready, 1)

            def pT1_half(t):
                dve.wait_ge(pT1_ps, t + 1)
                if t >= 2:
                    dve.wait_ge(m7_full, use["o1", t - 2] + 1)
                nc.vector.tensor_copy(pT1[:, t % 2, 4:8, :], psb(s1_bank(t) + 1).rearrange("p (h q) -> p h q", h=4)).then_inc(pT1b_ready, 1)

            def residual1(t):
                dve.wait_ge(m7_full, use["y1", t] + 1)
                dve.wait_ge(xbo_ready, 1)
                nc.vector.tensor_tensor(x1[:, t, :], ps[:, M7, P:2 * P], xbo[:, t, :], ALU.add).then_inc(m7_read, 1)

            def single(kind, b):
                k = use[kind, b]
                cols = slice(b * S, (b + 1) * S)
                tt = slice(2 * b, 2 * b + 2)
                if kind == "q2":
                    dve.wait_ge(qhi_ready, b + 1)
                    link(nc.vector.tensor_tensor(qres[:, cols], ps[:, M7, 0:S], qparts[:, 0, cols], ALU.subtract))
                    nc.vector.tensor_copy(qparts[:, 3, cols], qres[:, cols]).then_inc(qparts_ready, 1)
                    nc.vector.tensor_copy(qparts[:, 4, cols], qres[:, cols]).then_inc(qparts_ready, 1)
                    dve.wait_ge(qparts_ready, 2 * b + 1)
                    nc.vector.tensor_tensor(qparts[:, 5, cols], qres[:, cols], qparts[:, 3, cols], ALU.subtract).then_inc(m7_read, 1)
                if kind == "y2":
                    dve.wait_ge(m7_full, k + 1)
                    nc.vector.tensor_tensor(x2[:, tt, :], ps[:, M7, 0:S].rearrange("p (t d) -> p t d", t=2), x1[:, tt, :], ALU.add).then_inc(m7_read, 1)
                    dve.wait_ge(m7_read, k + 1)
                    moments(2, x2, tiles_of(b))
                if kind == "router":
                    dve.wait_ge(m7_full, k + 1)
                    br = xcol("br").unsqueeze(1).to_broadcast([P, 2, NE])
                    nc.vector.tensor_tensor(lg[:, tt, :], ps[:, M7, 0:2 * NE].rearrange("p (t e) -> p t e", e=NE), br, ALU.add).then_inc(m7_read, 1)
                    dve.wait_ge(m7_read, k + 1)
                    link(nc.vector.tensor_reduce(lmax[:, tt], lg[:, tt, :], AX.X, ALU.max))
                    nc.vector.tensor_tensor(lg[:, tt, :], lg[:, tt, :], lmax[:, tt].unsqueeze(2).to_broadcast([P, 2, NE]), ALU.subtract).then_inc(lg_ready, 1)
                if kind == "cwT":
                    dve.wait_ge(m7_full, k + 1)
                    nc.vector.tensor_copy(cwT[:, cols], ps[0:NE, M7, 0:S]).then_inc(m7_read, 1)
                if kind == "bias":
                    dve.wait_ge(m7_full, k + 1)
                    nc.vector.tensor_tensor(acc[:, tt, :], ps[:, M7, 0:S].rearrange("p (t d) -> p t d", t=2), x2[:, tt, :], ALU.add).then_inc(m7_read, 1)

            def top_two(b):
                tt = slice(2 * b, 2 * b + 2)
                dve.wait_ge(ex_ready, b + 1)
                link(nc.vector.tensor_reduce(esum[:, tt], ex[:, tt, :], AX.X, ALU.add))
                link(nc.vector.reciprocal(rsum[:, tt], esum[:, tt]))
                link(nc.vector.tensor_tensor(sc[:, tt, :], ex[:, tt, :], rsum[:, tt].unsqueeze(2).to_broadcast([P, 2, NE]), ALU.mult))
                for t in tiles_of(b):
                    last = nc.vector.max(top[:, t, :], sc[:, t, :])
                link(last)
                for t in tiles_of(b):
                    last = nc.vector.max_index(topi[:, t, :], top[:, t, :], sc[:, t, :])
                link(last)
                link(nc.vector.tensor_copy(topf[:, tt, :], topi[:, tt, :]))
                iota = xcol("iota").unsqueeze(1).to_broadcast([P, 2, NE])
                for k in range(2):
                    last = nc.vector.tensor_tensor(hit[:, k, tt, :], iota, topf[:, tt, k:k + 1].to_broadcast([P, 2, NE]), ALU.is_equal)
                link(last)
                for k in range(2):
                    last = nc.vector.tensor_tensor(hw[:, k, tt, :], hit[:, k, tt, :], top[:, tt, k:k + 1].to_broadcast([P, 2, NE]), ALU.mult)
                link(last)
                nc.vector.tensor_tensor(cw[:, tt, :], hw[:, 0, tt, :], hw[:, 1, tt, :], ALU.add).then_inc(cw_ready, 1)
                dve.wait_ge(cw_ready, b + 1)
                link(nc.vector.tensor_scalar(cwh[:, tt, :], cw[:, tt, :], 0.5, None, ALU.mult))

            maxima1(0)
            spread_keys(1)
            maxima1(1)
            context_keys()
            normalise_p(0)
            pT1_half(0)
            normalise_p(1)
            residual1(0)
            pT1_half(1)
            maxima1(2)
            residual1(1)
            dve.wait_ge(m7_read, use["y1", 1] + 1)
            moments(1, x1, tiles_of(0))
            normalise(1, x1, tiles_of(0), 2)
            maxima1(3)
            normalise_p(2)
            single("q2", 0)
            pT1_half(2)
            residual1(2)

            def split_max(u):
                b, quad = unit(u)
                m = m2[:, 2 * b:2 * b + 2, 4 * quad:4 * quad + 4].rearrange("p i (g s) -> p i s g", s=2)
                k = u % 2
                if u >= 2:
                    dve.wait_ge(m7_full, use["maxima", u - 2] + 1)
                link(nc.vector.tensor_scalar(nmq[:, k, :, :, 0, :], m, -1.0, None, ALU.mult))
                for i in range(2):
                    last = nc.vector.scalar_tensor_tensor(nmr[:, k, i, :, :], m[:, i, :, :], -1.0, nmq[:, k, i, :, 0, :], ALU.mult, ALU.subtract)
                link(last)
                link(nc.vector.tensor_copy(nmq[:, k, :, :, 1, :], nmr[:, k, :, :, :]))
                nc.vector.tensor_tensor(nmq[:, k, :, :, 2, :], nmr[:, k, :, :, :], nmq[:, k, :, :, 1, :], ALU.subtract).then_inc(nmq_ready, 1)

            def max_rows(u):
                dve.wait_ge(m7_full, use["maxima", u] + 1)
                if u >= 2:
                    dve.wait_ge(d_nm[u - 2], 16 * 2)
                nc.vector.tensor_copy(nmp[:, u % 2, :], ps[0:12, M7, 0:S]).then_inc(m7_read, 1)

            def head_outputs(u):
                b, quad = unit(u)
                dve.wait_ge(m7_full, use["outputs", u] + 1)
                o = ps[:, M7, 0:S].rearrange("p (i k c) -> p i k c", i=2, c=32)
                link(nc.vector.reciprocal(rs2[:, 2 * b:2 * b + 2, 4 * quad:4 * quad + 4], o[:, :, :, HD2]))
                nc.vector.tensor_tensor(o2[:, 2 * b:2 * b + 2, 32 * quad:32 * quad + 32].rearrange("p i (k d) -> p i k d", d=HD2),
                                        o[:, :, :, 0:HD2],
                                        rs2[:, 2 * b:2 * b + 2, 4 * quad:4 * quad + 4].unsqueeze(3).to_broadcast([P, 2, 4, HD2]),
                                        ALU.mult).then_inc(m7_read, 1)

            def expert_half(n):
                bias_g = w2[:, c2["gub"][0] + 4 * (n // NC % NE) + n % NC:c2["gub"][0] + 4 * (n // NC % NE) + n % NC + 1]
                dve.wait_ge(g_ps, n + 1)
                nc.vector.tensor_scalar(g1[:, n % 2, :], ps[:, n % 2, 0:S], bias_g, 7.0, ALU.add, ALU.min).then_inc(g1_ready, 1)
                dve.wait_ge(u1_ready, n + 1)
                nc.vector.tensor_scalar(u3[:, n % 2, :], u1[:, n % 2, :], -6.0, 8.0, ALU.max, ALU.min).then_inc(u3_ready, 1)
                if n >= 1:
                    activate(n - 1)

            def activate(n):
                m, c = n // NC, n % NC
                dve.wait_ge(gu3_ready, n + 1)
                dve.wait_ge(th_ready, n + 1)
                if m >= AHEAD and c == 0:
                    dve.wait_ge(dn_ps, m - AHEAD + 1)
                nc.vector.scalar_tensor_tensor(act_sb[:, m % AHEAD, c, :], th[:, n % 2, :], 1.0, gu3[:, n % 2, :], ALU.add, ALU.mult).then_inc(act_ready, 1)

            def combine(m):
                b, e = m // NE, m % NE
                dve.wait_ge(dn_ps, m + 1)
                if e == 0:
                    dve.wait_ge(m7_read, use["bias", b] + 1)
                else:
                    dve.wait_ge(dn_used, 2 * (m - b))
                for t in tiles_of(b):
                    nc.vector.scalar_tensor_tensor(acc[:, t, :], ps[:, 4 + m % 2, (t % 2) * D:(t % 2 + 1) * D], cwh[:, t, e:e + 1], acc[:, t, :],
                                                   ALU.mult, ALU.add).then_inc(acc_ready if e == NE - 1 else dn_used, 1)

            for g in range(LAST + 1):
                if g < STEPS:
                    b, quad = unit(g // 4)
                    qt, pair = 2 * b + g % 4 // 2, 2 * quad + g % 2
                    dve.wait_ge(s2_ps, g + 1)
                    nc.vector.tensor_reduce(m2[:, qt, 2 * pair:2 * pair + 2], ps[:, 2 * (g % 2):2 * (g % 2) + 2, :], AX.X, ALU.max).then_inc(m2_ready, 1)
                    if g % 4 == 3:
                        dve.wait_ge(m2_ready, g + 1)
                        split_max(g // 4)
                if g == 0:
                    normalise_p(3)
                    pT1_half(3)
                    residual1(3)
                    dve.wait_ge(m7_read, use["y1", 3] + 1)
                    moments(1, x1, tiles_of(1))
                if g == 1:
                    normalise(1, x1, tiles_of(1), 3)
                for kind, k in uses_at(g):
                    if kind == "maxima":
                        max_rows(k)
                    elif kind == "outputs":
                        head_outputs(k)
                    elif kind not in ("o1", "y1"):
                        single(kind, k)
                if g == 30:
                    normalise(2, x2, tiles_of(0), 4)
                if g == 34:
                    top_two(0)
                if FFN_FROM <= g < FFN_FROM + NC * AHEAD:
                    expert_half(g - FFN_FROM)
            for m in range(AHEAD, NX):
                for n in range(NC * m, NC * (m + 1)):
                    expert_half(n)
                for kind, b in LATE.get(m, []):
                    single(kind, b)
                    if kind == "y2":
                        normalise(2, x2, tiles_of(b), 5)
                    if kind == "router":
                        top_two(b)
                combine(m - AHEAD)
            activate(NX * NC - 1)
            for m in range(NX - AHEAD, NX):
                combine(m)

        @block.tensor
        def _(pe):
            mm = nc.tensor.matmul

            pe.wait_ge(d_w1, 16)
            for t in range(NT):
                pe.wait_ge(xn_ready, t + 1)
                last = nc.tensor.transpose(ps[:, 6, t * P:(t + 1) * P], xn[:, 0, t, :], identf)
            last.then_inc(xnT_ps, 1)
            pe.wait_ge(xnT_ready, 1)
            mm(psb(M7), wcol("wq"), xnT[:, 0, :], start=True, stop=True).then_inc(m7_full, 1)
            mm(psb(0), wcol("wk"), xnT[:, 0, :], start=True, stop=True).then_inc(qkv1_ps, 1)
            for t in range(NT):
                mm(ps[:, 5, t * P:(t + 1) * P], xnT[:, 0, t * P:(t + 1) * P], wcol("wv"), start=True, stop=True)
            for b in range(B):
                k0 = b * S + P - WIN
                last = mm(ps[0:WIN, 2, b * P:(b + 1) * P], xnT[:, 0, k0:k0 + WIN], wcol("wv"), start=True, stop=True)
            last.then_inc(qkv1_ps, 1)

            def context_keys():
                pe.wait_ge(d_ctx, 16)
                pe.wait_ge(d_w2, 16)
                pe.wait_ge(vpad_ready, B + NT)
                for c in range(2):
                    last = mm(psb(5 + c), xcol("wk"), ctx_sb[:, c * 512:(c + 1) * 512], start=True, stop=True)
                last.then_inc(kv2_ps, 1)

            def context_values():
                pe.wait_ge(kres_ready, 1)
                for k in range(B * NKT):
                    last = mm(ps[:, 5 + k // 4, (k % 4) * P:(k % 4 + 1) * P], ctx_sb[:, k * P:(k + 1) * P], xcol("wv"), start=True, stop=True)
                last.then_inc(kv2_ps, 1)

            def strip_scores(t):
                k, a = t % 2, s1_bank(t)
                key0 = (t // 2) * S + (P - WIN if k else 0)
                if t == 2:
                    pe.wait_ge(vaug_ready, 2)
                if t == 3:
                    pe.wait_ge(pT1a_ready, 2)
                    pe.wait_ge(pT1b_ready, 2)
                for i, (h0, h1) in enumerate(heads_of_bank(k)):
                    n = (h1 - h0) * STRIP[k]
                    mm(ps[:, a + i, 0:n], identb, mask_at[k][:, 0:n], start=True, stop=False)
                    last = mm(ps[:, a + i, 0:n].rearrange("p (h j) -> p h j", h=h1 - h0), qT[:, t * P:(t + 1) * P],
                              kexp[:, h0:h1, key0:key0 + STRIP[k]], start=False, stop=True)
                last.then_inc(s1_ps, 1)

            def strip_transposes(t):
                k, a = t % 2, s1_bank(t)
                pe.wait_ge(pn1_ready, t + 1)
                for h in range(H1):
                    last = nc.tensor.transpose(ps[:, a + h // 4, (h % 4) * P:(h % 4 + 1) * P], pn1[:, k, h, STRIP[k] - P:STRIP[k]], identf)
                last.then_inc(pT1_ps, 1)

            def strip_output(t):
                k = t % 2
                pe.wait_ge(pT1a_ready, t + 1)
                pe.wait_ge(pT1b_ready, t + 1)
                pe.wait_ge(m7_read, use["o1", t])
                if k == 1:
                    pe.wait_ge(spill_ready, t // 2 + 1)
                for odd in range(2):
                    for r in range(0, P, VC):
                        h = 2 * (r // VC) + odd
                        last = mm(ps[r:r + VC, M7, 0:P], vpad[:, t, h, :], pT1[:, k, h, :], start=not odd, stop=bool(odd) and k == 0)
                if k == 1:
                    for odd in range(2):
                        for r in range(0, P, VC):
                            h = 2 * (r // VC) + odd
                            last = mm(ps[r:r + VC, M7, 0:WIN], vspill[:, t // 2, h, :], pTs[:, h, :], start=False, stop=bool(odd))
                last.then_inc(m7_full, 1)
                pe.wait_ge(m7_read, use["y1", t])
                mm(ps[:, M7, P:2 * P], oT1[:, k, :], wcol("wo"), start=True, stop=True).then_inc(m7_full, 1)

            def single(kind, b):
                k = use[kind, b]
                pe.wait_ge(m7_read, k)
                two = range(2)
                at = lambda j: ps[:, M7, j * P:(j + 1) * P]
                if kind == "xn2":
                    pe.wait_ge(xn_ready, NT + 2 * b + 2)
                    last = [nc.tensor.transpose(at(j), xn[:, 1, 2 * b + j, :], identf) for j in two][-1]
                if kind == "q2":
                    last = mm(ps[:, M7, 0:S], xcol("wq"), xnT[:, 1, b * S:(b + 1) * S], start=True, stop=True)
                if kind == "maxima":
                    pe.wait_ge(nmq_ready, b + 1)
                    last = [mm(ps[0:12, M7, j * P:(j + 1) * P], nmq[:, b % 2, j, :, :, :].rearrange("p s j g -> p (s j g)"), identb,
                               start=True, stop=True) for j in two][-1]
                if kind == "outputs":
                    pe.wait_ge(oq_ready, b + 1)
                    last = [nc.tensor.transpose(at(j), oq[:, b % 2, j * P:(j + 1) * P], identf) for j in two][-1]
                if kind == "o2T":
                    last = [nc.tensor.transpose(at(j), o2[:, 2 * b + j, :], identf) for j in two][-1]
                if kind == "y2":
                    last = [mm(at(j), o2T[:, (2 * b + j) * P:(2 * b + j + 1) * P], xcol("wo"), start=True, stop=True) for j in two][-1]
                if kind == "xn3":
                    pe.wait_ge(xn_ready, 2 * NT + 2 * b + 2)
                    last = [nc.tensor.transpose(at(j), xn[:, 2, 2 * b + j, :], identf) for j in two][-1]
                if kind == "router":
                    last = [mm(ps[:, M7, j * NE:(j + 1) * NE], xnT[:, 2, (2 * b + j) * P:(2 * b + j + 1) * P], xcol("wr"), start=True, stop=True) for j in two][-1]
                if kind == "cwT":
                    pe.wait_ge(cw_ready, b + 1)
                    last = [nc.tensor.transpose(ps[0:NE, M7, j * P:(j + 1) * P], cw[:, 2 * b + j, :], identf) for j in two][-1]
                if kind == "bias":
                    pe.wait_ge(d_dn, 32)
                    last = [mm(at(j), cwT[:, (2 * b + j) * P:(2 * b + j + 1) * P], db_sb[:, :], start=True, stop=True) for j in two][-1]
                last.then_inc(m7_full, 1)

            pe.wait_ge(d_msk, 16)
            pe.wait_ge(m7_read, use["q1", 0] + 1)
            pe.wait_ge(kexp_ready, H1)
            strip_scores(0)
            pe.wait_ge(vpad_ready, B)
            strip_scores(1)
            context_keys()
            strip_transposes(0)
            strip_output(0)
            context_values()
            strip_transposes(1)
            strip_output(1)
            pe.wait_ge(kexp_ready, B * H1)
            strip_scores(2)
            single("xn2", 0)
            strip_scores(3)
            single("q2", 0)
            strip_transposes(2)
            strip_output(2)

            def row_scores(g):
                b, quad = unit(g // 4)
                qt, pair = g % 4 // 2, 2 * quad + g % 2
                if g >= 2:
                    pe.wait_ge(m2_ready, g - 1)
                else:
                    pe.wait_ge(pT1a_ready, 3 + g)
                    pe.wait_ge(pT1b_ready, 3 + g)
                for s in range(2):
                    last = mm(psb(2 * (g % 2) + s), qst[:, pair, b, s, qt * P:(qt + 1) * P], kst[:, pair, b * SK:(b + 1) * SK], start=True, stop=True)
                last.then_inc(s2_ps, 1)

            def key_scores(g):
                b, quad = unit(g // 4)
                k0 = b * SK + g % 4 * P
                for pair in range(2):
                    n = 2 * g + pair
                    if n >= 2:
                        pe.wait_ge(p2_ready, n - 1)
                    mm(psb(4 + n % 2), kst[:, 2 * quad + pair, k0:k0 + P], qst[:, 2 * quad + pair, b, :, :],
                       start=True, stop=True).then_inc(st_ps, 1)

            def weighted_values(g):
                b, quad = unit(g // 4)
                step = g % 4
                if step == 0:
                    if g >= 4:
                        pe.wait_ge(oq_ready, g // 4)
                pe.wait_ge(p2_ready, 2 * g + 2)
                for k in range(4):
                    last = mm(ps[32 * k:32 * k + 32, 6, 0:S], vaug[:, b * NKT + step, 4 * quad + k, :], pT2[:, g % RING, k, :],
                              start=(step == 0), stop=(step == NKT - 1))
                last.then_inc(pv_step, 1)

            def up(n):
                m, c = n // NC, n % NC
                b, e = m // NE, m % NE
                if n >= 2:
                    pe.wait_ge(g1_ready, n - 1)
                else:
                    pe.wait_ge(m2_ready, STEPS)
                mm(ps[:, n % 2, 0:S], gu_sb[:, e, c * P:(c + 1) * P], xnT[:, 2, b * S:(b + 1) * S], start=True, stop=True).then_inc(g_ps, 1)
                if n >= 2:
                    pe.wait_ge(u1_ready, n - 1)
                mm(ps[:, 2 + n % 2, 0:S], gu_sb[:, e, FI + c * P:FI + (c + 1) * P], xnT[:, 2, b * S:(b + 1) * S], start=True, stop=True).then_inc(u_ps, 1)

            def down(m):
                b, e = m // NE, m % NE
                pe.wait_ge(act_ready, NC * (m + 1))
                if m >= 2:
                    if (m - 2) % NE == NE - 1:
                        pe.wait_ge(acc_ready, 2 * ((m - 2) // NE + 1))
                    else:
                        pe.wait_ge(dn_used, 2 * (m - 1 - (m - 2) // NE))
                for j in range(2):
                    for c in range(NC):
                        last = mm(ps[:, 4 + m % 2, j * D:(j + 1) * D], act_sb[:, m % AHEAD, c, j * P:(j + 1) * P], dn_sb[:, e, c, :],
                                  start=(c == 0), stop=(c == NC - 1))
                last.then_inc(dn_ps, 1)

            for g in range(LAST + 1):
                if g < STEPS:
                    if g % 4 == 0:
                        pe.wait_ge(d_qst[g // 4], 16 * 4)
                        pe.wait_ge(d_kst[g // 4 % QUADS], 16 * 4)
                    row_scores(g)
                if g == 0:
                    strip_transposes(3)
                    strip_output(3)
                for kind, k in uses_at(g):
                    if kind not in ("o1", "y1"):
                        single(kind, k)
                if LAG2 <= g < STEPS + LAG2:
                    if g % 4 == 0:
                        pe.wait_ge(d_nm[(g - LAG2) // 4], 16 * 2)
                    key_scores(g - LAG2)
                if LAG2 + LAGV <= g < STEPS + LAG2 + LAGV:
                    weighted_values(g - LAG2 - LAGV)
                if g == FFN_FROM:
                    pe.wait_ge(d_gu, 16)
                if FFN_FROM <= g < FFN_FROM + NC * AHEAD:
                    up(g - FFN_FROM)
            pe.wait_ge(d_dn, 32)
            for m in range(AHEAD, NX):
                late = LATE.get(m, [])
                if late:
                    single(*late[0])
                down(m - AHEAD)
                up(NC * m)
                up(NC * m + 1)
                for kind, b in late[1:]:
                    single(kind, b)
            for m in range(NX - AHEAD, NX):
                down(m)


def kernel(**inputs):
    import ml_dtypes
    import concourse.bacc as bacc
    from concourse.bass_utils import run_bass_kernel_spmd

    a = {k: np.asarray(v) for k, v in inputs.items()}
    f32 = np.float32
    rows = lambda v: np.broadcast_to(v.reshape(1, -1), (P, v.size))
    heads = np.zeros((P, H1), f32)
    for h in range(H1):
        heads[h * HD1:(h + 1) * HD1, h] = 1
    rep = lambda w: np.repeat(w.reshape(KV, 1, HD1, -1), H1 // KV, axis=1).reshape(P, -1)
    pack1 = dict(wq=a["L0_attn_Wq"].T, wk=rep(a["L0_attn_Wk"]).T, wv=rep(a["L0_attn_Wv"]).T, wo=a["L0_attn_Wo"].T,
                 ident=np.eye(P, dtype=f32), bq=a["L0_attn_bq"].reshape(P, 1), bk=rep(a["L0_attn_bk"]),
                 sink=rows(a["L0_attn_sink_bias"]), bv=rows(rep(a["L0_attn_bv"])), bo=rows(a["L0_attn_bo"]), head=heads)
    pack2 = dict(wq=a["L0_xattn_Wq"].T, wk=a["L0_xattn_Wk"].T, wv=a["L0_xattn_Wv"].T, wo=a["L0_xattn_Wo"].T,
                 wr=a["L0_ffn_router_weight"].T, br=rows(a["L0_ffn_router_bias"]),
                 gub=a["L0_ffn_gate_up_bias"].reshape(4 * NE, P).T, iota=rows(np.arange(NE, dtype=f32)))
    q, j = np.arange(P)[:, None], np.arange(STRIP[1])[None, :]
    first = (j[:, :P] <= q) & (j[:, :P] > q - WIN)
    second = (j - WIN <= q) & (j > q)
    masks = [np.tile(np.where(ok, 0.0, MASKED), (1, n)) for ok, n in ((first, HB[0]), (second, HB[1]))]
    maskc = np.concatenate(masks + [np.eye(P)], axis=1).astype(ml_dtypes.bfloat16)
    arrays = dict(
        x=a["x"].reshape(T, D), ctxT=a["ctx_1024"].reshape(B * SK, D).T,
        pack1=np.concatenate([pack1[k] for k in PACK1], axis=1), pack2=np.concatenate([pack2[k] for k in PACK2], axis=1),
        maskc=maskc, gu=a["L0_ffn_gate_up_proj"], dn=a["L0_ffn_down_proj"], db=a["L0_ffn_down_bias"])
    arrays = {k: np.ascontiguousarray(v) for k, v in arrays.items()}

    nc = bacc.Bacc("TRN2", target_bir_lowering=False, num_devices=1)
    args = [nc.dram_tensor(k, v.shape, mybir.dt.from_np(v.dtype), kind="ExternalInput").ap() for k, v in arrays.items()]
    out = nc.dram_tensor("out", (T, D), mybir.dt.float32, kind="ExternalOutput").ap()
    build(nc, *args, out)
    r = run_bass_kernel_spmd(nc, [arrays], core_ids=[0])
    return r.results[0]["out"].reshape(B, S, D)
```

```python
import numpy as np
import concourse.bass as bass
from concourse import mybir
from contextlib import ExitStack

P = 128
B, S, D = 2, 256, 128
T = B * S
NT = T // P
SK = 512
NKT = SK // P
H1, KV, HD1, WIN = 8, 2, 16, 32
H2, HD2 = 16, 8
NE, FI = 8, 256
NC = FI // P
TERMS = 6
SLOTS = 8
STACK = HD2 * SLOTS
NPAIR = H2 // 2
QUADS = 4
UNITS = B * QUADS
STEPS = 4 * UNITS
LAG2 = 8
LAGV = 2
RING = 4
LAST = STEPS + LAG2 + LAGV + 1
NX = B * NE
AHEAD = 4
FFN_FROM = STEPS
EPS = 1e-5
ONES2 = float(np.uint32(0x3F803F80).view(np.float32))
MASKED = -1e30
STRIP = (P, P + WIN)
HB = (4, 3)
VC = 2 * HD1

PACK1 = dict(ident=P, wq=P, wk=P, wv=P, bq=1, bk=1, sink=1, head=H1, wo=P, bv=P, bo=D)
PACK2 = dict(wq=P, wk=P, wv=P, wo=P, wr=NE, br=NE, gub=4 * NE, iota=NE)


def columns(pack):
    at, out = 0, {}
    for name, n in pack.items():
        out[name] = (at, at + n)
        at += n
    return out, at


def build(nc, x, ctxT, pack1, pack2, maskc, gu, dn, db, out):
    fp32, bf16, u32 = mybir.dt.float32, mybir.dt.bfloat16, mybir.dt.uint32
    ALU, ACT, AX = mybir.AluOpType, mybir.ActivationFunctionType, mybir.AxisListType
    c1, n1 = columns(PACK1)
    c2, n2 = columns(PACK2)

    with ExitStack() as ctx:
        def sb(name, shape, dt=fp32):
            return ctx.enter_context(nc.sbuf_tensor(name, shape, dt))

        def sem(name):
            return ctx.enter_context(nc.semaphore(name))

        xs = sb("xs", [P, NT, D])
        xbo = sb("xbo", [P, NT, D])
        w1 = sb("w1", [P, n1])
        w2 = sb("w2", [P, n2])
        msk = sb("msk", [P, 4 * P + 3 * STRIP[1] + P], bf16)
        ctx_sb = sb("ctx_sb", [P, B * SK])
        db_sb = sb("db_sb", [NE, D])
        stats = sb("stats", [P, 3, NT, 6])
        mv = sb("mv", [P, 3, NT, 2])
        veps = sb("veps", [P, 3, NT])
        mhalf = sb("mhalf", [P, 2])
        rstd = sb("rstd", [P, 3, NT])
        xn = sb("xn", [P, 3, NT, D])
        xnT = sb("xnT", [P, 3, T])
        qT = sb("qT", [P, T])
        kT = sb("kT", [P, T])
        vpad = sb("vpad", [P, NT, H1, VC])
        vspill = sb("vspill", [WIN, B, H1, VC])
        negm1 = sb("negm1", [P, NT, H1])
        rmax1 = sb("rmax1", [P, NT, H1])
        sums1 = sb("sums1", [P, NT, H1])
        esink = sb("esink", [P, NT, H1])
        den1 = sb("den1", [P, NT, H1])
        rden1 = sb("rden1", [P, NT, H1])
        pT1 = sb("pT1", [P, 2, H1, P])
        pTs = sb("pTs", [WIN, H1, WIN])
        oT1 = sb("oT1", [P, 2, P])
        x1 = sb("x1", [P, NT, D])
        kparts = sb("kparts", [P, SLOTS, B * SK], bf16)
        qparts = sb("qparts", [P, SLOTS, T], bf16)
        kst = sb("kst", [P, NPAIR, B * SK], bf16)
        qst = sb("qst", [P, NPAIR, B, 2, S], bf16)
        vaug = sb("vaug", [P, B * NKT, H2, 32])
        m2 = sb("m2", [P, NT, H2])
        nmf = sb("nmf", [P, 2, 2, 2])
        nmr = sb("nmr", [P, 2, 2, 2])
        nmq = sb("nmq", [P, 2, 2, 2, HD2, 2], bf16)
        nmp = sb("nmp", [4 * HD2, 2, S], bf16)
        pT2 = sb("pT2", [P, RING, 4, S])
        kres = pT2[:, :, :, :].rearrange("p a b c -> p (a b c)")[:, 2 * H1 * STRIP[1]:2 * H1 * STRIP[1] + B * SK]
        pn1 = pT2[:, :, :, :].rearrange("p a b c -> p (a b c)")[:, 0:2 * H1 * STRIP[1]].rearrange("p (n h j) -> p n h j", n=2, h=H1)
        big = sb("big", [P, 14 * T])
        oq = sb("oq", [P, 2, S])
        rs2 = sb("rs2", [P, NT, H2])
        o2 = xs
        o2T = sb("o2T", [P, T])
        x2 = sb("x2", [P, NT, D])
        lg = sb("lg", [P, NT, NE])
        lmax = sb("lmax", [P, NT])
        ex = sb("ex", [P, NT, NE])
        esum = sb("esum", [P, NT])
        rsum = sb("rsum", [P, NT])
        sc = sb("sc", [P, NT, NE])
        top = sb("top", [P, NT, 8])
        topi = sb("topi", [P, NT, 8], u32)
        topf = sb("topf", [P, NT, 8])
        hit = sb("hit", [P, 2, NT, NE])
        hw = sb("hw", [P, 2, NT, NE])
        cw = sb("cw", [P, NT, NE])
        cwT = sb("cwT", [NE, T])
        cwh = sb("cwh", [P, NT, NE])
        bup = sb("bup", [P, 4 * NE])
        spare = big
        g1, th, u1, u3, gu3 = (spare[:, 2 * S * k:2 * S * (k + 1)].rearrange("p (n t) -> p n t", n=2) for k in range(5))
        act_sb = spare[:, 10 * S:10 * S + AHEAD * NC * S].rearrange("p (n c t) -> p n c t", n=AHEAD, c=NC)
        qres = spare[:, H1 * T + 2 * H1 * STRIP[1]:H1 * T + 2 * H1 * STRIP[1] + T]
        kexp = spare[:, 0:H1 * T].rearrange("p (h t) -> p h t", h=H1)
        p1 = spare[:, H1 * T:H1 * T + 2 * H1 * STRIP[1]].rearrange("p (n h j) -> p n h j", n=2, h=H1)
        wexp = sb("wexp", [P, NE * 2 * FI + NE * NC * D])
        gu_sb = wexp[:, 0:NE * 2 * FI].rearrange("p (e n) -> p e n", e=NE)
        dn_sb = wexp[:, NE * 2 * FI:].rearrange("p (e c d) -> p e c d", e=NE, c=NC)
        acc = xbo

        wcol = lambda name: w1[:, c1[name][0]:c1[name][1]]
        xcol = lambda name: w2[:, c2[name][0]:c2[name][1]]
        identf = wcol("ident")
        mask_at = (msk[:, 0:4 * P], msk[:, 4 * P:4 * P + 3 * STRIP[1]])
        identb = msk[:, 4 * P + 3 * STRIP[1]:]

        ps = ctx.enter_context(nc.psum_tensor("ps", [P, 8, 512], fp32))
        psb = lambda b: ps[:, b, :]

        d_x, d_w1, d_msk, d_ctx, d_w2, d_gu, d_dn = (sem(n) for n in
                                                     ("d_x", "d_w1", "d_msk", "d_ctx", "d_w2", "d_gu", "d_dn"))
        d_kst = [sem(f"d_kst{u}") for u in range(QUADS)]
        d_qst = [sem(f"d_qst{k}") for k in range(B * NPAIR)]
        d_nm = [sem(f"d_nm{u}") for u in range(UNITS)]
        d_out = sem("d_out")
        zeroed = sem("zeroed")
        ones_ready = sem("ones_ready")
        vzeroed = sem("vzeroed")
        chain = sem("chain")
        pchain = sem("pchain")
        kmid_ready = sem("kmid_ready")
        var_ready, rstd_ready, xn_ready, xbo_ready = sem("var_ready"), sem("rstd_ready"), sem("xn_ready"), sem("xbo_ready")
        xnT_ps, xnT_ready = sem("xnT_ps"), sem("xnT_ready")
        kv2_ps = sem("kv2_ps")
        khi_ready, kres_ready, kparts_ready, vaug_ready = (sem("khi_ready"), sem("kres_ready"), sem("kparts_ready"), sem("vaug_ready"))
        kv1_ps = sem("kv1_ps")
        kT_ready, kexp_ready, vpad_ready = sem("kT_ready"), sem("kexp_ready"), sem("vpad_ready")
        s1_ps, negm1_ready, p1_ready, esink_ready, pn1_ready = (sem("s1_ps"), sem("negm1_ready"), sem("p1_ready"), sem("esink_ready"), sem("pn1_ready"))
        spill_ready = sem("spill_ready")
        pT1_ps, pT1a_ready, pT1b_ready = sem("pT1_ps"), sem("pT1a_ready"), sem("pT1b_ready")
        qhi_ready, qparts_ready = sem("qhi_ready"), sem("qparts_ready")
        s2_ps, m2_ready = sem("s2_ps"), sem("m2_ready")
        gu3_ready, th_ready, u3_ready, bup_ready = sem("gu3_ready"), sem("th_ready"), sem("u3_ready"), sem("bup_ready")
        nmq_ready = sem("nmq_ready")
        m7_full, m7_read = sem("m7_full"), sem("m7_read")
        st_ps, p2_ready = sem("st_ps"), sem("p2_ready")
        pv_step, oq_ready = sem("pv_step"), sem("oq_ready")
        lg_ready, ex_ready, cw_ready = sem("lg_ready"), sem("ex_ready"), sem("cw_ready")
        acc_ready = sem("acc_ready")
        g_ps, u_ps, g1_ready, u1_ready = sem("g_ps"), sem("u_ps"), sem("g1_ready"), sem("u1_ready")
        act_ready, dn_ps, dn_used = sem("act_ready"), sem("dn_ps"), sem("dn_used")

        block = ctx.enter_context(nc.Block())
        turned_at = lambda g: (g - LAG2 - LAGV - 4) // 4 if g >= LAG2 + LAGV + 4 and (g - LAG2 - LAGV) % 4 == 0 else None

        TILE3_TURN, TILE3_OUT = 2, 3
        BACKGROUND = {5: ("xn2", 1), 6: ("q2", 1), 27: ("o2T", 0), 28: ("y2", 0), 31: ("xn3", 0), 32: ("router", 0), 35: ("cwT", 0), 36: ("bias", 0)}
        Y2_STEP, ROUTER_STEP = (g for g in sorted(BACKGROUND) if BACKGROUND[g][0] in ("y2", "router"))

        def uses_at(g):
            out = [("o1", 3), ("y1", 3)] if g == TILE3_OUT else []
            if g % 4 == 1 and 4 <= g < STEPS + 4:
                out.append(("maxima", g // 4 - 1))
            if turned_at(g) is not None:
                out.append(("outputs", turned_at(g)))
            return out + ([BACKGROUND[g]] if g in BACKGROUND else [])

        chunk_at = {**{FFN_FROM + n: n for n in range(NC * AHEAD)}, **{40: 8, 41: 9, 43: 10}}
        CHUNKS_IN_STEPS = len(chunk_at)
        LATE = {11: ("o2T", 1), 12: ("y2", 1), 15: ("xn3", 1), 19: ("router", 1), 23: ("cwT", 1), 25: ("bias", 1)}
        Y2_CHUNK, ROUTER_CHUNK = (n for n in sorted(LATE) if LATE[n][0] in ("y2", "router"))
        USES = ([("q1", 0), ("o1", 0), ("y1", 0), ("q1", 1), ("o1", 1), ("y1", 1), ("v1", 1), ("xn2", 0), ("q2", 0), ("o1", 2), ("y1", 2)]
                + [u for g in range(LAST + 1) for u in uses_at(g)] + [LATE[n] for n in sorted(LATE)])
        use = {u: k for k, u in enumerate(USES)}
        heads_of_bank = lambda k: [(i, min(i + HB[k], H1)) for i in range(0, H1, HB[k])]
        s1_bank = lambda t: (0, 2, 0, 4)[t]
        s2_bank = lambda g: 2 - 2 * (g % 2)
        XNT_BANK, K_BANK = (6, 3), (4, 2)
        M7 = 7
        unit = lambda u: (u // QUADS, u % QUADS)

        @block.sync
        def _(sp):
            sp.dma_start(xs[:, :, :], x.rearrange("(t p) d -> p t d", p=P)).then_inc(d_x, 16)
            sp.dma_start(w1[:, :], pack1).then_inc(d_w1, 16)
            sp.dma_start(msk[:, :], maskc).then_inc(d_msk, 16)
            sp.dma_start(gu_sb[:, :, :], gu.rearrange("e p n -> p e n")).then_inc(d_gu, 16)
            sp.dma_start(dn_sb[:, :, :, :], dn.rearrange("e (c p) d -> p e c d", p=P)).then_inc(d_dn, 16)
            sp.dma_start(db_sb[:, :], db).then_inc(d_dn, 16)
            sp.wait_ge(khi_ready, 2)
            sp.wait_ge(kmid_ready, 1)
            sp.wait_ge(kparts_ready, 4)
            sp.wait_ge(ones_ready, 1)
            for pair in range(NPAIR):
                sp.dma_start(kst[:, pair, :], kparts[2 * pair * HD2:2 * (pair + 1) * HD2, :, :]).then_inc(d_kst[pair // 2], 16)

            def stack_queries(b, pairs):
                sp.wait_ge(qparts_ready, 2 * (b + 1))
                sp.wait_ge(m7_read, use["q2", b] + 1)
                sp.wait_ge(ones_ready, 2)
                sp.wait_ge(zeroed, 4)
                for pair in pairs:
                    for s in range(2):
                        h = 2 * pair + s
                        sp.dma_start(qst[STACK * s:STACK * (s + 1), pair, b, s, :],
                                     qparts[h * HD2:(h + 1) * HD2, :, b * S:(b + 1) * S]).then_inc(d_qst[b * NPAIR + pair], 16)

            def stack_maxima(u):
                b, quad = unit(u)
                sp.wait_ge(m7_read, use["maxima", u] + 1)
                for s in range(2):
                    sp.dma_start(qst[STACK * s + TERMS:STACK * (s + 1):SLOTS, 2 * quad:2 * quad + 2, b, s, :],
                                 nmp[2 * HD2 * s:2 * HD2 * (s + 1), u % 2, :]).then_inc(d_nm[u], 16)

            stack_queries(0, range(NPAIR))
            stack_maxima(0)
            stack_maxima(1)
            stack_queries(1, range(0, 4))
            stack_maxima(2)
            stack_queries(1, range(4, NPAIR))
            for u in range(3, UNITS):
                stack_maxima(u)
            for b in range(B):
                sp.wait_ge(acc_ready, 2 * (b + 1))
                sp.dma_start(out[b * S:(b + 1) * S, :].rearrange("(t p) d -> p t d", p=P), acc[:, 2 * b:2 * b + 2, :]).then_inc(d_out, 16)
            sp.wait_ge(d_out, 16 * B)

        def split_max(pool, u):
            b, quad = unit(u)
            m = m2[:, 2 * b:2 * b + 2, 4 * quad:4 * quad + 4].rearrange("p i (g s) -> p i s g", s=2)
            k = u % 2
            pool.wait_ge(m2_ready, 4 * (u + 1))
            if u == 0:
                pool.wait_ge(ones_ready, 3)
            if u >= 2:
                pool.wait_ge(m7_full, use["maxima", u - 2] + 1)
            nc.gpsimd.tensor_scalar(nmf[:, :, :, :], m, -1.0, None, ALU.mult).then_inc(pchain, 1)
            pool.wait_ge(pchain, 4 * u + 1)
            nc.gpsimd.tensor_copy(nmq[:, k, :, :, 0, :], nmf[:, :, :, :]).then_inc(pchain, 1)
            pool.wait_ge(pchain, 4 * u + 2)
            nc.gpsimd.tensor_tensor(nmr[:, :, :, :], nmf[:, :, :, :], nmq[:, k, :, :, 0, :], ALU.subtract).then_inc(pchain, 1)
            pool.wait_ge(pchain, 4 * u + 3)
            nc.gpsimd.tensor_copy(nmq[:, k, :, :, 1, :], nmr[:, :, :, :]).then_inc(pchain, 1)
            pool.wait_ge(pchain, 4 * u + 4)
            nc.gpsimd.tensor_tensor(nmq[:, k, :, :, 2, :], nmr[:, :, :, :], nmq[:, k, :, :, 1, :], ALU.subtract).then_inc(nmq_ready, 1)

        def gate_times_up(pool, n):
            pool.wait_ge(g1_ready, n + 1)
            pool.wait_ge(u3_ready, n + 1)
            if n >= 2:
                pool.wait_ge(act_ready, n - 1)
            nc.gpsimd.tensor_tensor(gu3[:, n % 2, :], g1[:, n % 2, :], u3[:, n % 2, :], ALU.mult).then_inc(gu3_ready, 1)

        @block.gpsimd
        def _(pool):
            nc.gpsimd.memset(mhalf[:, :], -0.5).then_inc(zeroed, 1)
            nc.gpsimd.memset(vaug[:, :, :, :], 0.0).then_inc(zeroed, 1)
            pool.wait_ge(zeroed, 2)
            for b in range(B):
                pool.wait_ge(var_ready, b + 1)
                nc.gpsimd.tensor_tensor(rstd[:, 0, 2 * b:2 * b + 2], veps[:, 0, 2 * b:2 * b + 2], mhalf[:, 0:2], ALU.pow).then_inc(rstd_ready, 1)
            nc.gpsimd.memset(vaug[:, :, :, HD2:HD2 + 1], 1.0).then_inc(zeroed, 1)
            nc.gpsimd.memset(kparts[:, TERMS:SLOTS, :].rearrange("p a b -> p (a b)").bitcast(fp32), ONES2).then_inc(ones_ready, 1)
            nc.gpsimd.memset(qparts[:, TERMS:SLOTS, :].rearrange("p a b -> p (a b)").bitcast(fp32), 0.0).then_inc(ones_ready, 1)
            nc.gpsimd.memset(nmq[:, :, :, :, :, :].rearrange("p a b c d e -> p (a b c d e)").bitcast(fp32), 0.0).then_inc(ones_ready, 1)
            nc.gpsimd.memset(qst[:, :, :, :, :].rearrange("p a b c d -> p (a b c d)").bitcast(fp32), 0.0).then_inc(zeroed, 1)
            pool.wait_ge(d_x, 16)
            pool.wait_ge(d_w1, 16)
            nc.gpsimd.tensor_tensor(xbo[:, :, :], xs[:, :, :], wcol("bo").unsqueeze(1).to_broadcast([P, NT, D]), ALU.add).then_inc(xbo_ready, 1)
            pool.wait_ge(kres_ready, 1)
            nc.gpsimd.tensor_copy(kparts[:, 1, :], kres[:, :]).then_inc(kmid_ready, 1)
            nc.gpsimd.tensor_copy(kparts[:, 4, :], kres[:, :]).then_inc(kparts_ready, 1)
            pool.wait_ge(kmid_ready, 1)
            nc.gpsimd.tensor_tensor(kparts[:, 2, :], kres[:, :], kparts[:, 1, :], ALU.subtract).then_inc(kparts_ready, 1)
            pool.wait_ge(d_w2, 16)
            nc.gpsimd.tensor_scalar(bup[:, :], xcol("gub"), 1.0, None, ALU.add).then_inc(bup_ready, 1)
            for k, (n, b) in enumerate(((1, 0), (1, 1), (2, 0), (2, 1))):
                if k == 1:
                    split_max(pool, 0)
                if k == 2:
                    for u in range(1, UNITS - 1):
                        split_max(pool, u)
                if k == 3:
                    split_max(pool, UNITS - 1)
                    for chunk in range(Y2_CHUNK):
                        gate_times_up(pool, chunk)
                pool.wait_ge(var_ready, B + 1 + k)
                nc.gpsimd.tensor_tensor(rstd[:, n, 2 * b:2 * b + 2], veps[:, n, 2 * b:2 * b + 2], mhalf[:, 0:2], ALU.pow).then_inc(rstd_ready, 1)
            for n in range(Y2_CHUNK, NX * NC):
                gate_times_up(pool, n)

        @block.scalar
        def _(act):
            act.dma_start(ctx_sb[:, :], ctxT).then_inc(d_ctx, 16)
            act.dma_start(w2[:, :], pack2).then_inc(d_w2, 16)
            for b in range(B):
                act.wait_ge(xnT_ps, b + 1)
                nc.scalar.activation(xnT[:, 0, b * S:(b + 1) * S], ps[:, XNT_BANK[b], 0:S], ACT.Copy).then_inc(xnT_ready, 1)
            for b in range(B):
                act.wait_ge(kv1_ps, 2 * b + 1)
                nc.scalar.activation(kT[:, b * S:(b + 1) * S], ps[:, K_BANK[b], 0:S], ACT.Identity, bias=wcol("bk")).then_inc(kT_ready, 1)
            def context_keys():
                act.wait_ge(kv2_ps, 1)
                for c in range(2):
                    nc.scalar.activation(kparts[:, 0, c * 512:(c + 1) * 512], psb(5 + c), ACT.Copy).then_inc(khi_ready, 1)

            def high_parts():
                act.wait_ge(khi_ready, 2)
                for j, term in enumerate((3, 5)):
                    nc.scalar.activation(kparts[:, term, :], kparts[:, 0, :], ACT.Copy).then_inc(kparts_ready, 1)

            def context_values():
                act.wait_ge(kv2_ps, 2)
                act.wait_ge(zeroed, 3)
                for c in range(2):
                    nc.scalar.activation(vaug[:, 4 * c:4 * c + 4, :, 0:HD2],
                                         psb(5 + c).rearrange("p (t h d) -> p t h d", t=4, d=HD2), ACT.Copy).then_inc(vaug_ready, 1)

            def softmax1(t):
                k = t % 2
                act.wait_ge(negm1_ready, t + 1)
                for i, (h0, h1) in enumerate(heads_of_bank(k)):
                    for h in range(h0, h1):
                        src = ps[:, s1_bank(t) + i, (h - h0) * STRIP[k]:(h - h0 + 1) * STRIP[k]]
                        if t >= 2 and h == 0:
                            act.wait_ge(pn1_ready, t - 1)
                        nc.scalar.activation(p1[:, k, h, 0:STRIP[k]], src, ACT.Exp, bias=negm1[:, t, h:h + 1],
                                             accum_out=sums1[:, t, h:h + 1]).then_inc(p1_ready, 1)
                nc.scalar.activation(esink[:, t, :], negm1[:, t, :], ACT.Exp, bias=wcol("sink")).then_inc(esink_ready, 1)

            def pT1_half(t):
                act.wait_ge(pT1_ps, t + 1)
                if t >= 2:
                    act.wait_ge(m7_full, use["o1", t - 2] + 1)
                nc.scalar.activation(pT1[:, t % 2, 0:4, :], psb(s1_bank(t)).rearrange("p (h q) -> p h q", h=4), ACT.Copy).then_inc(pT1a_ready, 1)

            def turn1(t):
                act.wait_ge(m7_full, use["o1", t] + 1)
                nc.scalar.activation(oT1[:, t % 2, :], ps[:, M7, 0:P], ACT.Copy).then_inc(m7_read, 1)

            def single(kind, b):
                k = use[kind, b]
                cols = slice(b * S, (b + 1) * S)
                if kind in ("xn2", "o2T", "xn3"):
                    dst = {"xn2": xnT[:, 1, cols], "o2T": o2T[:, cols], "xn3": xnT[:, 2, cols]}[kind]
                    act.wait_ge(m7_full, k + 1)
                    nc.scalar.activation(dst, ps[:, M7, 0:S], ACT.Copy).then_inc(m7_read, 1)
                if kind == "q2":
                    act.wait_ge(m7_full, k + 1)
                    nc.scalar.activation(qparts[:, 0:3, cols], ps[:, M7, 0:S].unsqueeze(1).to_broadcast([P, 3, S]), ACT.Copy).then_inc(qhi_ready, 1)
                if kind == "router":
                    act.wait_ge(lg_ready, b + 1)
                    nc.scalar.activation(ex[:, 2 * b:2 * b + 2, :], lg[:, 2 * b:2 * b + 2, :], ACT.Exp).then_inc(ex_ready, 1)

            softmax1(0)
            context_keys()
            softmax1(1)
            pT1_half(0)
            turn1(0)
            high_parts()
            pT1_half(1)
            turn1(1)
            context_values()
            single("xn2", 0)
            single("q2", 0)
            softmax1(2)
            softmax1(3)
            pT1_half(2)
            turn1(2)

            def exponentials(g):
                if g >= RING:
                    act.wait_ge(pv_step, g - RING + 1)
                for pair in range(2):
                    n = 2 * g + pair
                    act.wait_ge(st_ps, n + 1)
                    nc.scalar.activation(pT2[:, g % RING, 2 * pair:2 * pair + 2, :],
                                         psb(4 + n % 2).rearrange("p (s q) -> p s q", s=2), ACT.Exp,
                                         scale=float(HD2) ** -0.5).then_inc(p2_ready, 1)

            def out_quad(u):
                act.wait_ge(pv_step, 4 * u + 4)
                if u >= 2:
                    act.wait_ge(m7_full, use["outputs", u - 2] + 1)
                nc.scalar.activation(oq[:, u % 2, :], ps[:, 6, 0:S], ACT.Copy).then_inc(oq_ready, 1)

            def max_rows(u):
                act.wait_ge(m7_full, use["maxima", u] + 1)
                if u >= 2:
                    act.wait_ge(d_nm[u - 2], 16 * 2)
                nc.scalar.activation(nmp[:, u % 2, :], ps[0:4 * HD2, M7, 0:S], ACT.Copy).then_inc(m7_read, 1)

            def expert_half(n):
                bias_u = bup[:, 4 * (n // NC % NE) + NC + n % NC:4 * (n // NC % NE) + NC + n % NC + 1]
                act.wait_ge(u_ps, n + 1)
                if n == 0:
                    act.wait_ge(bup_ready, 1)
                if n >= 2:
                    act.wait_ge(u3_ready, n - 1)
                nc.scalar.activation(u1[:, n % 2, :], ps[:, 2 + n % 2, 0:S], ACT.Identity, bias=bias_u).then_inc(u1_ready, 1)
                act.wait_ge(g1_ready, n + 1)
                if n >= 2:
                    act.wait_ge(act_ready, n - 1)
                nc.scalar.activation(th[:, n % 2, :], g1[:, n % 2, :], ACT.Tanh, scale=0.5 * 1.702).then_inc(th_ready, 1)

            for g in range(LAST + 1):
                for kind, k in uses_at(g):
                    if kind == "maxima":
                        max_rows(k)
                if LAG2 <= g < STEPS + LAG2:
                    exponentials(g - LAG2)
                if g == TILE3_TURN:
                    pT1_half(3)
                if g == TILE3_OUT:
                    turn1(3)
                if g >= LAG2 + LAGV and (g - LAG2 - LAGV) % 4 == 3:
                    out_quad((g - LAG2 - LAGV) // 4)
                for kind, k in uses_at(g):
                    if kind not in ("maxima", "outputs", "o1", "y1"):
                        single(kind, k)
                if g in chunk_at:
                    expert_half(chunk_at[g])
            for n in range(CHUNKS_IN_STEPS, NX * NC):
                if n in LATE:
                    single(*LATE[n])
                expert_half(n)

        @block.vector
        def _(dve):
            links = [0]

            def link(ins):
                links[0] += 1
                ins.then_inc(chain, 1)
                dve.wait_ge(chain, links[0])

            def moments(n, src, tiles):
                for t in tiles:
                    links[0] += 1
                    nc.vector.bn_stats(stats[:, n, t, :], src[:, t, :]).then_inc(chain, 1)
                dve.wait_ge(chain, links[0])
                for t in tiles:
                    last = nc.vector.bn_aggr(mv[:, n, t, :], stats[:, n, t, :])
                link(last)
                tt = slice(tiles[0], tiles[-1] + 1)
                nc.vector.tensor_scalar(veps[:, n, tt], mv[:, n, tt, 1], EPS, None, ALU.add).then_inc(var_ready, 1)

            def normalise(n, src, tiles, k):
                dve.wait_ge(rstd_ready, k)
                for t in tiles:
                    nc.vector.tensor_scalar(xn[:, n, t, :], src[:, t, :], mv[:, n, t, 0:1], rstd[:, n, t:t + 1],
                                            ALU.subtract, ALU.mult).then_inc(xn_ready, 1)


            tiles_of = lambda b: range(2 * b, 2 * b + 2)
            nc.vector.memset(vpad[:, :, :, :], 0.0).then_inc(vzeroed, 1)
            nc.vector.memset(vspill[:, :, :, :], 0.0).then_inc(vzeroed, 1)
            dve.wait_ge(d_x, 16)
            for b in range(B):
                moments(0, xs, tiles_of(b))
            for b in range(B):
                normalise(0, xs, tiles_of(b), b + 1)

            def queries1(b):
                cols = slice(b * S, (b + 1) * S)
                dve.wait_ge(m7_full, use["q1", b] + 1)
                nc.vector.tensor_scalar(qT[:, cols], ps[:, M7, 0:S], wcol("bq"), float(HD1) ** -0.5, ALU.add, ALU.mult).then_inc(m7_read, 1)

            def spread_keys(b):
                cols = slice(b * S, (b + 1) * S)
                dve.wait_ge(kT_ready, b + 1)
                for h in range(H1):
                    nc.vector.tensor_scalar(kexp[:, h, cols], kT[:, cols], w1[:, c1["head"][0] + h:c1["head"][0] + h + 1], None, ALU.mult).then_inc(kexp_ready, 1)

            by_pair = lambda v: v.rearrange("p h c -> p (h c)").rearrange("p (g k d) -> p g k d", k=4, d=HD1)[:, :, 0:4:3, :]
            rows = lambda v: v.rearrange("p (g r d) -> p g r d", r=2, d=HD1)

            def spread_values(b, bank):
                nc.vector.tensor_tensor(by_pair(vspill[:, b, :, :]), rows(ps[0:WIN, bank, 2 * P:3 * P]), rows(wcol("bv")[0:WIN]), ALU.add).then_inc(vpad_ready, 1)
                for j in range(2):
                    last = nc.vector.tensor_tensor(by_pair(vpad[:, 2 * b + j, :, :]), rows(ps[:, bank, j * P:(j + 1) * P]), rows(wcol("bv")), ALU.add)
                    last.then_inc(vpad_ready if j == 0 or bank != M7 else m7_read, 1)

            dve.wait_ge(d_w1, 16)
            queries1(0)
            spread_keys(0)
            dve.wait_ge(kv1_ps, 2)
            dve.wait_ge(vzeroed, 2)
            spread_values(0, 5)

            def context_keys():
                dve.wait_ge(khi_ready, 2)
                link(nc.vector.tensor_tensor(kres[:, 0:512], psb(5), kparts[:, 0, 0:512], ALU.subtract))
                nc.vector.tensor_tensor(kres[:, 512:1024], psb(6), kparts[:, 0, 512:1024], ALU.subtract).then_inc(kres_ready, 1)

            def maxima1(t):
                k = t % 2
                dve.wait_ge(s1_ps, t + 1)
                if k == 0:
                    link(nc.vector.tensor_reduce(rmax1[:, t, :], ps[:, s1_bank(t):s1_bank(t) + 2, :].rearrange("p b (h j) -> p (b h) j", h=4), AX.X, ALU.max))
                else:
                    a = s1_bank(t)
                    nc.vector.tensor_reduce(rmax1[:, t, 0:6].rearrange("p (b h) -> p b h", b=2),
                                            ps[:, a:a + 2, 0:3 * STRIP[1]].rearrange("p b (h j) -> p b h j", h=3), AX.X, ALU.max)
                    link(nc.vector.tensor_reduce(rmax1[:, t, 6:8], ps[:, a + 2, 0:2 * STRIP[1]].rearrange("p (h j) -> p h j", h=2), AX.X, ALU.max))
                nc.vector.tensor_scalar(negm1[:, t, :], rmax1[:, t, :], wcol("sink"), -1.0, ALU.max, ALU.mult).then_inc(negm1_ready, 1)

            def normalise_p(t):
                k = t % 2
                dve.wait_ge(p1_ready, H1 * (t + 1))
                dve.wait_ge(esink_ready, t + 1)
                link(nc.vector.tensor_tensor(den1[:, t, :], sums1[:, t, :], esink[:, t, :], ALU.add))
                link(nc.vector.reciprocal(rden1[:, t, :], den1[:, t, :]))
                if t >= 2:
                    dve.wait_ge(pT1_ps, t - 1)
                nc.vector.tensor_tensor(pn1[:, k, :, 0:STRIP[k]], p1[:, k, :, 0:STRIP[k]],
                                        rden1[:, t, :].unsqueeze(2).to_broadcast([P, H1, STRIP[k]]), ALU.mult).then_inc(pn1_ready, 1)
                if k == 1:
                    dve.wait_ge(pn1_ready, t + 1)
                    if t == 3:
                        dve.wait_ge(m7_full, use["o1", 1] + 1)
                    nc.vector.transpose(pTs[:, :, :], pn1[0:WIN, 1, :, 0:WIN]).then_inc(spill_ready, 1)

            def pT1_half(t):
                dve.wait_ge(pT1_ps, t + 1)
                if t >= 2:
                    dve.wait_ge(m7_full, use["o1", t - 2] + 1)
                nc.vector.tensor_copy(pT1[:, t % 2, 4:8, :], psb(s1_bank(t) + 1).rearrange("p (h q) -> p h q", h=4)).then_inc(pT1b_ready, 1)

            def residual1(t):
                dve.wait_ge(m7_full, use["y1", t] + 1)
                dve.wait_ge(xbo_ready, 1)
                nc.vector.tensor_tensor(x1[:, t, :], ps[:, M7, P:2 * P], xbo[:, t, :], ALU.add).then_inc(m7_read, 1)

            def single(kind, b):
                k = use[kind, b]
                cols = slice(b * S, (b + 1) * S)
                tt = slice(2 * b, 2 * b + 2)
                if kind == "q2":
                    dve.wait_ge(qhi_ready, b + 1)
                    link(nc.vector.tensor_tensor(qres[:, cols], ps[:, M7, 0:S], qparts[:, 0, cols], ALU.subtract))
                    nc.vector.tensor_copy(qparts[:, 3, cols], qres[:, cols]).then_inc(qparts_ready, 1)
                    nc.vector.tensor_copy(qparts[:, 4, cols], qres[:, cols]).then_inc(qparts_ready, 1)
                    dve.wait_ge(qparts_ready, 2 * b + 1)
                    nc.vector.tensor_tensor(qparts[:, 5, cols], qres[:, cols], qparts[:, 3, cols], ALU.subtract).then_inc(m7_read, 1)
                if kind == "y2":
                    dve.wait_ge(m7_full, k + 1)
                    nc.vector.tensor_tensor(x2[:, tt, :], ps[:, M7, 0:S].rearrange("p (t d) -> p t d", t=2), x1[:, tt, :], ALU.add).then_inc(m7_read, 1)
                    dve.wait_ge(m7_read, k + 1)
                    moments(2, x2, tiles_of(b))
                if kind == "router":
                    dve.wait_ge(m7_full, k + 1)
                    br = xcol("br").unsqueeze(1).to_broadcast([P, 2, NE])
                    nc.vector.tensor_tensor(lg[:, tt, :], ps[:, M7, 0:2 * NE].rearrange("p (t e) -> p t e", e=NE), br, ALU.add).then_inc(m7_read, 1)
                    dve.wait_ge(m7_read, k + 1)
                    link(nc.vector.tensor_reduce(lmax[:, tt], lg[:, tt, :], AX.X, ALU.max))
                    nc.vector.tensor_tensor(lg[:, tt, :], lg[:, tt, :], lmax[:, tt].unsqueeze(2).to_broadcast([P, 2, NE]), ALU.subtract).then_inc(lg_ready, 1)
                if kind == "cwT":
                    dve.wait_ge(m7_full, k + 1)
                    nc.vector.tensor_copy(cwT[:, cols], ps[0:NE, M7, 0:S]).then_inc(m7_read, 1)
                if kind == "bias":
                    dve.wait_ge(m7_full, k + 1)
                    nc.vector.tensor_tensor(acc[:, tt, :], ps[:, M7, 0:S].rearrange("p (t d) -> p t d", t=2), x2[:, tt, :], ALU.add).then_inc(m7_read, 1)

            def top_two(b):
                tt = slice(2 * b, 2 * b + 2)
                dve.wait_ge(ex_ready, b + 1)
                link(nc.vector.tensor_reduce(esum[:, tt], ex[:, tt, :], AX.X, ALU.add))
                link(nc.vector.reciprocal(rsum[:, tt], esum[:, tt]))
                link(nc.vector.tensor_tensor(sc[:, tt, :], ex[:, tt, :], rsum[:, tt].unsqueeze(2).to_broadcast([P, 2, NE]), ALU.mult))
                for t in tiles_of(b):
                    last = nc.vector.max(top[:, t, :], sc[:, t, :])
                link(last)
                for t in tiles_of(b):
                    last = nc.vector.max_index(topi[:, t, :], top[:, t, :], sc[:, t, :])
                link(last)
                link(nc.vector.tensor_copy(topf[:, tt, :], topi[:, tt, :]))
                iota = xcol("iota").unsqueeze(1).to_broadcast([P, 2, NE])
                for k in range(2):
                    last = nc.vector.tensor_tensor(hit[:, k, tt, :], iota, topf[:, tt, k:k + 1].to_broadcast([P, 2, NE]), ALU.is_equal)
                link(last)
                for k in range(2):
                    last = nc.vector.tensor_tensor(hw[:, k, tt, :], hit[:, k, tt, :], top[:, tt, k:k + 1].to_broadcast([P, 2, NE]), ALU.mult)
                link(last)
                nc.vector.tensor_tensor(cw[:, tt, :], hw[:, 0, tt, :], hw[:, 1, tt, :], ALU.add).then_inc(cw_ready, 1)
                dve.wait_ge(cw_ready, b + 1)
                link(nc.vector.tensor_scalar(cwh[:, tt, :], cw[:, tt, :], 0.5, None, ALU.mult))

            maxima1(0)
            spread_keys(1)
            maxima1(1)
            context_keys()
            normalise_p(0)
            pT1_half(0)
            normalise_p(1)
            residual1(0)
            queries1(1)
            pT1_half(1)
            residual1(1)
            dve.wait_ge(m7_read, use["y1", 1] + 1)
            moments(1, x1, tiles_of(0))
            dve.wait_ge(m7_full, use["v1", 1] + 1)
            spread_values(1, M7)
            normalise(1, x1, tiles_of(0), 3)
            maxima1(2)
            single("q2", 0)

            def head_outputs(u):
                b, quad = unit(u)
                dve.wait_ge(m7_full, use["outputs", u] + 1)
                o = ps[:, M7, 0:S].rearrange("p (i k c) -> p i k c", i=2, c=32)
                link(nc.vector.reciprocal(rs2[:, 2 * b:2 * b + 2, 4 * quad:4 * quad + 4], o[:, :, :, HD2]))
                nc.vector.tensor_tensor(o2[:, 2 * b:2 * b + 2, 32 * quad:32 * quad + 32].rearrange("p i (k d) -> p i k d", d=HD2),
                                        o[:, :, :, 0:HD2],
                                        rs2[:, 2 * b:2 * b + 2, 4 * quad:4 * quad + 4].unsqueeze(3).to_broadcast([P, 2, 4, HD2]),
                                        ALU.mult).then_inc(m7_read, 1)

            def expert_half(n):
                bias_g = w2[:, c2["gub"][0] + 4 * (n // NC % NE) + n % NC:c2["gub"][0] + 4 * (n // NC % NE) + n % NC + 1]
                dve.wait_ge(g_ps, n + 1)
                nc.vector.tensor_scalar(g1[:, n % 2, :], ps[:, n % 2, 0:S], bias_g, 7.0, ALU.add, ALU.min).then_inc(g1_ready, 1)
                dve.wait_ge(u1_ready, n + 1)
                nc.vector.tensor_scalar(u3[:, n % 2, :], u1[:, n % 2, :], -6.0, 8.0, ALU.max, ALU.min).then_inc(u3_ready, 1)
                if n >= 1:
                    activate(n - 1)

            def expert_chunk(n):
                expert_half(n)
                if n % NC == NC - 1 and n // NC >= AHEAD:
                    combine(n // NC - AHEAD)

            def activate(n):
                m, c = n // NC, n % NC
                dve.wait_ge(gu3_ready, n + 1)
                dve.wait_ge(th_ready, n + 1)
                if m >= AHEAD and c == 0:
                    dve.wait_ge(dn_ps, m - AHEAD + 1)
                nc.vector.scalar_tensor_tensor(act_sb[:, m % AHEAD, c, :], th[:, n % 2, :], 1.0, gu3[:, n % 2, :], ALU.add, ALU.mult).then_inc(act_ready, 1)

            def combine(m):
                b, e = m // NE, m % NE
                dve.wait_ge(dn_ps, m + 1)
                if e == 0:
                    dve.wait_ge(m7_read, use["bias", b] + 1)
                else:
                    dve.wait_ge(dn_used, 2 * (m - b))
                for t in tiles_of(b):
                    nc.vector.scalar_tensor_tensor(acc[:, t, :], ps[:, 4 + m % 2, (t % 2) * D:(t % 2 + 1) * D], cwh[:, t, e:e + 1], acc[:, t, :],
                                                   ALU.mult, ALU.add).then_inc(acc_ready if e == NE - 1 else dn_used, 1)

            def row_maxima(g):
                b, quad = unit(g // 4)
                qt, pair = 2 * b + g % 4 // 2, 2 * quad + g % 2
                dve.wait_ge(s2_ps, g + 1)
                nc.vector.tensor_reduce(m2[:, qt, 2 * pair:2 * pair + 2], ps[:, s2_bank(g):s2_bank(g) + 2, :], AX.X, ALU.max).then_inc(m2_ready, 1)

            maxima1(3)
            normalise_p(2)
            row_maxima(0)
            pT1_half(2)
            normalise_p(3)
            residual1(2)
            for g in range(LAST + 1):
                if 1 <= g < STEPS:
                    row_maxima(g)
                if g == TILE3_TURN:
                    pT1_half(3)
                if g == TILE3_OUT:
                    residual1(3)
                    dve.wait_ge(m7_read, use["y1", 3] + 1)
                    moments(1, x1, tiles_of(1))
                if g == TILE3_OUT + 1:
                    normalise(1, x1, tiles_of(1), 4)
                for kind, k in uses_at(g):
                    if kind == "outputs":
                        head_outputs(k)
                    elif kind not in ("o1", "y1", "maxima"):
                        single(kind, k)
                if g == Y2_STEP + 1:
                    normalise(2, x2, tiles_of(0), 5)
                if g == ROUTER_STEP + 1:
                    top_two(0)
                if g in chunk_at:
                    expert_chunk(chunk_at[g])
            for n in range(CHUNKS_IN_STEPS, NX * NC):
                if n in LATE:
                    single(*LATE[n])
                expert_chunk(n)
                if n == Y2_CHUNK:
                    normalise(2, x2, tiles_of(1), 6)
                if n == ROUTER_CHUNK:
                    top_two(1)
            activate(NX * NC - 1)
            for m in range(NX - AHEAD, NX):
                combine(m)

        @block.tensor
        def _(pe):
            mm = nc.tensor.matmul
            cols = lambda b: slice(b * S, (b + 1) * S)

            def queries1(b):
                pe.wait_ge(m7_read, use["q1", b])
                mm(ps[:, M7, 0:S], wcol("wq"), xnT[:, 0, cols(b)], start=True, stop=True).then_inc(m7_full, 1)

            def keys1(b):
                pe.wait_ge(xnT_ready, b + 1)
                mm(ps[:, K_BANK[b], 0:S], wcol("wk"), xnT[:, 0, cols(b)], start=True, stop=True).then_inc(kv1_ps, 1)

            def values1(b, bank):
                for j in range(2):
                    t = 2 * b + j
                    mm(ps[:, bank, j * P:(j + 1) * P], xnT[:, 0, t * P:(t + 1) * P], wcol("wv"), start=True, stop=True)
                k0 = b * S + P - WIN
                return mm(ps[0:WIN, bank, 2 * P:3 * P], xnT[:, 0, k0:k0 + WIN], wcol("wv"), start=True, stop=True)

            pe.wait_ge(d_w1, 16)
            for b in range(B):
                for t in range(2 * b, 2 * b + 2):
                    pe.wait_ge(xn_ready, t + 1)
                    last = nc.tensor.transpose(ps[:, XNT_BANK[b], t % 2 * P:(t % 2 + 1) * P], xn[:, 0, t, :], identf)
                last.then_inc(xnT_ps, 1)
            keys1(0)
            queries1(0)
            values1(0, 5).then_inc(kv1_ps, 1)
            keys1(1)

            def context_keys():
                pe.wait_ge(d_ctx, 16)
                pe.wait_ge(d_w2, 16)
                pe.wait_ge(vpad_ready, 3)
                for c in range(2):
                    last = mm(psb(5 + c), xcol("wk"), ctx_sb[:, c * 512:(c + 1) * 512], start=True, stop=True)
                last.then_inc(kv2_ps, 1)

            def context_values():
                pe.wait_ge(kres_ready, 1)
                for k in range(B * NKT):
                    last = mm(ps[:, 5 + k // 4, (k % 4) * P:(k % 4 + 1) * P], ctx_sb[:, k * P:(k + 1) * P], xcol("wv"), start=True, stop=True)
                last.then_inc(kv2_ps, 1)

            def strip_scores(t, part=(0, 1, 2)):
                k, a = t % 2, s1_bank(t)
                key0 = (t // 2) * S + (P - WIN if k else 0)
                pe.wait_ge(m7_read, use["q1", t // 2] + 1)
                if t == 2:
                    pe.wait_ge(pT1a_ready, 1)
                    pe.wait_ge(pT1b_ready, 1)
                if t == 3:
                    pe.wait_ge(p1_ready, 2 * H1)
                    pe.wait_ge(vaug_ready, 2)
                for i, (h0, h1) in enumerate(heads_of_bank(k)):
                    if i not in part:
                        continue
                    n = (h1 - h0) * STRIP[k]
                    mm(ps[:, a + i, 0:n], identb, mask_at[k][:, 0:n], start=True, stop=False)
                    last = mm(ps[:, a + i, 0:n].rearrange("p (h j) -> p h j", h=h1 - h0), qT[:, t * P:(t + 1) * P],
                              kexp[:, h0:h1, key0:key0 + STRIP[k]], start=False, stop=True)
                    if h1 == H1:
                        last.then_inc(s1_ps, 1)

            def strip_transposes(t):
                k, a = t % 2, s1_bank(t)
                pe.wait_ge(pn1_ready, t + 1)
                for h in range(H1):
                    last = nc.tensor.transpose(ps[:, a + h // 4, (h % 4) * P:(h % 4 + 1) * P], pn1[:, k, h, STRIP[k] - P:STRIP[k]], identf)
                last.then_inc(pT1_ps, 1)

            def strip_output(t):
                k = t % 2
                pe.wait_ge(pT1a_ready, t + 1)
                pe.wait_ge(pT1b_ready, t + 1)
                pe.wait_ge(m7_read, use["o1", t])
                if k == 1:
                    pe.wait_ge(spill_ready, t // 2 + 1)
                for odd in range(2):
                    for r in range(0, P, VC):
                        h = 2 * (r // VC) + odd
                        last = mm(ps[r:r + VC, M7, 0:P], vpad[:, t, h, :], pT1[:, k, h, :], start=not odd, stop=bool(odd) and k == 0)
                if k == 1:
                    for odd in range(2):
                        for r in range(0, P, VC):
                            h = 2 * (r // VC) + odd
                            last = mm(ps[r:r + VC, M7, 0:WIN], vspill[:, t // 2, h, :], pTs[:, h, :], start=False, stop=bool(odd))
                last.then_inc(m7_full, 1)
                pe.wait_ge(m7_read, use["y1", t])
                mm(ps[:, M7, P:2 * P], oT1[:, k, :], wcol("wo"), start=True, stop=True).then_inc(m7_full, 1)

            def single(kind, b):
                k = use[kind, b]
                pe.wait_ge(m7_read, k)
                two = range(2)
                at = lambda j: ps[:, M7, j * P:(j + 1) * P]
                if kind == "xn2":
                    pe.wait_ge(xn_ready, NT + 2 * b + 2)
                    last = [nc.tensor.transpose(at(j), xn[:, 1, 2 * b + j, :], identf) for j in two][-1]
                if kind == "q2":
                    last = mm(ps[:, M7, 0:S], xcol("wq"), xnT[:, 1, b * S:(b + 1) * S], start=True, stop=True)
                if kind == "maxima":
                    pe.wait_ge(nmq_ready, b + 1)
                    last = [mm(ps[0:4 * HD2, M7, j * P:(j + 1) * P], nmq[:, b % 2, j, :, :, :].rearrange("p s j g -> p (s j g)"), identb,
                               start=True, stop=True) for j in two][-1]
                if kind == "outputs":
                    pe.wait_ge(oq_ready, b + 1)
                    last = [nc.tensor.transpose(at(j), oq[:, b % 2, j * P:(j + 1) * P], identf) for j in two][-1]
                if kind == "o2T":
                    last = [nc.tensor.transpose(at(j), o2[:, 2 * b + j, :], identf) for j in two][-1]
                if kind == "y2":
                    last = [mm(at(j), o2T[:, (2 * b + j) * P:(2 * b + j + 1) * P], xcol("wo"), start=True, stop=True) for j in two][-1]
                if kind == "xn3":
                    pe.wait_ge(xn_ready, 2 * NT + 2 * b + 2)
                    last = [nc.tensor.transpose(at(j), xn[:, 2, 2 * b + j, :], identf) for j in two][-1]
                if kind == "router":
                    last = [mm(ps[:, M7, j * NE:(j + 1) * NE], xnT[:, 2, (2 * b + j) * P:(2 * b + j + 1) * P], xcol("wr"), start=True, stop=True) for j in two][-1]
                if kind == "cwT":
                    pe.wait_ge(cw_ready, b + 1)
                    last = [nc.tensor.transpose(ps[0:NE, M7, j * P:(j + 1) * P], cw[:, 2 * b + j, :], identf) for j in two][-1]
                if kind == "bias":
                    pe.wait_ge(d_dn, 32)
                    last = [mm(at(j), cwT[:, (2 * b + j) * P:(2 * b + j + 1) * P], db_sb[:, :], start=True, stop=True) for j in two][-1]
                last.then_inc(m7_full, 1)

            pe.wait_ge(d_msk, 16)
            pe.wait_ge(m7_read, use["q1", 0] + 1)
            pe.wait_ge(kexp_ready, H1)
            strip_scores(0)
            pe.wait_ge(kT_ready, B)
            strip_scores(1)
            context_keys()
            strip_transposes(0)
            strip_output(0)
            strip_transposes(1)
            queries1(1)
            context_values()
            strip_output(1)
            pe.wait_ge(m7_read, use["v1", 1])
            values1(1, M7).then_inc(m7_full, 1)
            pe.wait_ge(kexp_ready, B * H1)
            strip_scores(2, (0,))
            single("xn2", 0)
            strip_scores(2, (1,))
            single("q2", 0)
            strip_scores(3)

            def row_scores(g):
                b, quad = unit(g // 4)
                qt, pair = g % 4 // 2, 2 * quad + g % 2
                if g % 4 == 0:
                    pe.wait_ge(d_kst[quad], 16 * 2)
                if g % 4 < 2:
                    pe.wait_ge(d_qst[b * NPAIR + pair], 16 * 2)
                if g >= 2:
                    pe.wait_ge(m2_ready, g - 1)
                else:
                    pe.wait_ge(pT1a_ready, 2 + g)
                    pe.wait_ge(pT1b_ready, 2 + g)
                for s in range(2):
                    last = mm(psb(s2_bank(g) + s), qst[:, pair, b, s, qt * P:(qt + 1) * P], kst[:, pair, b * SK:(b + 1) * SK], start=True, stop=True)
                last.then_inc(s2_ps, 1)

            def key_scores(g):
                b, quad = unit(g // 4)
                k0 = b * SK + g % 4 * P
                for pair in range(2):
                    n = 2 * g + pair
                    if n >= 2:
                        pe.wait_ge(p2_ready, n - 1)
                    else:
                        pe.wait_ge(pT1a_ready, NT)
                        pe.wait_ge(pT1b_ready, NT)
                    mm(psb(4 + n % 2), kst[:, 2 * quad + pair, k0:k0 + P], qst[:, 2 * quad + pair, b, :, :],
                       start=True, stop=True).then_inc(st_ps, 1)

            def weighted_values(g):
                b, quad = unit(g // 4)
                step = g % 4
                if step == 0 and g >= 4:
                    pe.wait_ge(oq_ready, g // 4)
                pe.wait_ge(p2_ready, 2 * g + 2)
                for k in range(4):
                    last = mm(ps[32 * k:32 * k + 32, 6, 0:S], vaug[:, b * NKT + step, 4 * quad + k, :], pT2[:, g % RING, k, :],
                              start=(step == 0), stop=(step == NKT - 1))
                last.then_inc(pv_step, 1)

            def up(n):
                m, c = n // NC, n % NC
                b, e = m // NE, m % NE
                if n % (NC * NE) == 0:
                    pe.wait_ge(m7_read, use["xn3", b] + 1)
                if n >= 2:
                    pe.wait_ge(g1_ready, n - 1)
                else:
                    pe.wait_ge(m2_ready, STEPS)
                mm(ps[:, n % 2, 0:S], gu_sb[:, e, c * P:(c + 1) * P], xnT[:, 2, b * S:(b + 1) * S], start=True, stop=True).then_inc(g_ps, 1)
                if n >= 2:
                    pe.wait_ge(u1_ready, n - 1)
                mm(ps[:, 2 + n % 2, 0:S], gu_sb[:, e, FI + c * P:FI + (c + 1) * P], xnT[:, 2, b * S:(b + 1) * S], start=True, stop=True).then_inc(u_ps, 1)

            def down(m):
                b, e = m // NE, m % NE
                pe.wait_ge(act_ready, NC * (m + 1))
                if m < 2:
                    pe.wait_ge(d_dn, 32)
                    pe.wait_ge(p2_ready, 2 * STEPS)
                if m >= 2:
                    if (m - 2) % NE == NE - 1:
                        pe.wait_ge(acc_ready, 2 * ((m - 2) // NE + 1))
                    else:
                        pe.wait_ge(dn_used, 2 * (m - 1 - (m - 2) // NE))
                for j in range(2):
                    for c in range(NC):
                        last = mm(ps[:, 4 + m % 2, j * D:(j + 1) * D], act_sb[:, m % AHEAD, c, j * P:(j + 1) * P], dn_sb[:, e, c, :],
                                  start=(c == 0), stop=(c == NC - 1))
                last.then_inc(dn_ps, 1)

            def chunk(n):
                if n % NC == 0 and n // NC >= AHEAD:
                    down(n // NC - AHEAD)
                up(n)

            row_scores(0)
            strip_transposes(2)
            strip_output(2)
            for g in range(LAST + 1):
                if 1 <= g < STEPS:
                    row_scores(g)
                for kind, k in uses_at(g):
                    if kind == "maxima":
                        single(kind, k)
                if g == TILE3_TURN:
                    strip_transposes(3)
                if g == TILE3_OUT:
                    strip_output(3)
                if LAG2 <= g < STEPS + LAG2:
                    if (g - LAG2) % 4 == 0:
                        pe.wait_ge(d_nm[(g - LAG2) // 4], 16 * 2)
                    key_scores(g - LAG2)
                if LAG2 + LAGV <= g < STEPS + LAG2 + LAGV:
                    weighted_values(g - LAG2 - LAGV)
                for kind, k in uses_at(g):
                    if kind not in ("o1", "y1", "maxima"):
                        single(kind, k)
                if g == FFN_FROM:
                    pe.wait_ge(d_gu, 16)
                if g in chunk_at:
                    chunk(chunk_at[g])
            for n in range(CHUNKS_IN_STEPS, NX * NC):
                if n in LATE:
                    single(*LATE[n])
                chunk(n)
            for m in range(NX - AHEAD, NX):
                down(m)


def kernel(**inputs):
    import ml_dtypes
    import concourse.bacc as bacc
    from concourse.bass_utils import run_bass_kernel_spmd

    a = {k: np.asarray(v) for k, v in inputs.items()}
    f32 = np.float32
    rows = lambda v: np.broadcast_to(v.reshape(1, -1), (P, v.size))
    heads = np.zeros((P, H1), f32)
    for h in range(H1):
        heads[h * HD1:(h + 1) * HD1, h] = 1
    rep = lambda w: np.repeat(w.reshape(KV, 1, HD1, -1), H1 // KV, axis=1).reshape(P, -1)
    pack1 = dict(wq=a["L0_attn_Wq"].T, wk=rep(a["L0_attn_Wk"]).T, wv=rep(a["L0_attn_Wv"]).T, wo=a["L0_attn_Wo"].T,
                 ident=np.eye(P, dtype=f32), bq=a["L0_attn_bq"].reshape(P, 1), bk=rep(a["L0_attn_bk"]),
                 sink=rows(a["L0_attn_sink_bias"]), bv=rows(rep(a["L0_attn_bv"])), bo=rows(a["L0_attn_bo"]), head=heads)
    pack2 = dict(wq=a["L0_xattn_Wq"].T, wk=a["L0_xattn_Wk"].T, wv=a["L0_xattn_Wv"].T, wo=a["L0_xattn_Wo"].T,
                 wr=a["L0_ffn_router_weight"].T, br=rows(a["L0_ffn_router_bias"]),
                 gub=a["L0_ffn_gate_up_bias"].reshape(4 * NE, P).T, iota=rows(np.arange(NE, dtype=f32)))
    q, j = np.arange(P)[:, None], np.arange(STRIP[1])[None, :]
    first = (j[:, :P] <= q) & (j[:, :P] > q - WIN)
    second = (j - WIN <= q) & (j > q)
    masks = [np.tile(np.where(ok, 0.0, MASKED), (1, n)) for ok, n in ((first, HB[0]), (second, HB[1]))]
    maskc = np.concatenate(masks + [np.eye(P)], axis=1).astype(ml_dtypes.bfloat16)
    arrays = dict(
        x=a["x"].reshape(T, D), ctxT=a["ctx_1024"].reshape(B * SK, D).T,
        pack1=np.concatenate([pack1[k] for k in PACK1], axis=1), pack2=np.concatenate([pack2[k] for k in PACK2], axis=1),
        maskc=maskc, gu=a["L0_ffn_gate_up_proj"], dn=a["L0_ffn_down_proj"], db=a["L0_ffn_down_bias"])
    arrays = {k: np.ascontiguousarray(v) for k, v in arrays.items()}

    nc = bacc.Bacc("TRN2", target_bir_lowering=False, num_devices=1)
    args = [nc.dram_tensor(k, v.shape, mybir.dt.from_np(v.dtype), kind="ExternalInput").ap() for k, v in arrays.items()]
    out = nc.dram_tensor("out", (T, D), mybir.dt.float32, kind="ExternalOutput").ap()
    build(nc, *args, out)
    r = run_bass_kernel_spmd(nc, [arrays], core_ids=[0])
    return r.results[0]["out"].reshape(B, S, D)
```
